# Optimizing a Trainium2 kernel written in Bass

```python
import numpy as np
import jax
import jax.numpy as jnp

def _softmax(x, axis=-1):
    return jax.nn.softmax(x, axis=axis)

def _gelu(x):
    return jax.nn.gelu(x, approximate=True)

def _silu(x):
    return jax.nn.silu(x)

def _sigmoid(x):
    return jax.nn.sigmoid(x)

def _layernorm(x, axis=-1, eps=1e-05):
    m = jnp.mean(x, axis=axis, keepdims=True)
    v = jnp.var(x, axis=axis, keepdims=True)
    return (x - m) / jnp.sqrt(v + eps)

def _scatter_add(tgt, idx, src, axis=0):
    return tgt.at[idx].add(src)

def _segment_sum(src, seg, n):
    return jax.ops.segment_sum(src, seg, n)
kernel_name = 'mk_perceiver_d1_seqx_r2_a5fb83'

def setup_inputs(seed: int=0):
    np.random.seed(seed)
    _w = jnp.asarray

    def _rec_inputs():
        import jax
        import jax.numpy as jnp
        _rk = jax.random.key(seed)
        x = -0.000125 + 0.9999 * jax.random.normal(jax.random.fold_in(_rk, 1), (1, 256, 1024), jnp.float32)
        _lenS = 256 - jax.random.randint(jax.random.fold_in(_rk, 7), (1,), 0, max(1, 256 // 4) + 1, jnp.int32)
        _lenS2 = 25088 - jax.random.randint(jax.random.fold_in(_rk, 8), (1,), 0, max(1, 25088 // 4) + 1, jnp.int32)
        _ctx_2048P = jax.random.normal(jax.random.fold_in(_rk, 11), (1, 16, 1024), jnp.float32)
        _ctx_2048c = jax.random.dirichlet(jax.random.fold_in(_rk, 511), 0.3 * jnp.ones((16,), jnp.float32), (1, 25088))
        _ctx_2048t = jnp.einsum('bsk,bkd->bsd', _ctx_2048c, _ctx_2048P)
        _ctx_2048t = _ctx_2048t * jax.lax.rsqrt(jnp.mean(jnp.square(_ctx_2048t)) + 1e-12) * 0.953939
        ctx_2048 = -0.000514642 + 1.00011 * (_ctx_2048t + 0.3 * jax.random.normal(jax.random.fold_in(_rk, 611), (1, 25088, 1024), jnp.float32))
        _validS = jnp.arange(256)[None, :] < _lenS[:, None]
        _validS2 = jnp.arange(25088)[None, :] < _lenS2[:, None]
        _causal = jnp.tril(jnp.ones((256, 256), dtype=bool))
        mask_BxS2_bk0 = jnp.logical_not(jnp.broadcast_to(_validS2[:, :], (1, 25088)))
        return (x, ctx_2048, mask_BxS2_bk0)
    x, ctx_2048, mask_BxS2_bk0 = _rec_inputs()

    def _L0_xattn_setup():
        import jax, jax.numpy as jnp
        import numpy as np
        key = jax.random.key(seed)
        k1, k2, k3 = jax.random.split(key, 3)
        B, S, D, M = (8, 1024, 1024, 128)
        hidden_states = jax.random.normal(k1, (B, S, D), dtype=jnp.float32)
        memory_tokens = jax.random.normal(k2, (B, M, D), dtype=jnp.float32)
        memory_mask = jax.random.randint(k3, (B, M), 0, 2).astype(jnp.bool_)
        return {'hidden_states': hidden_states, 'memory_tokens': memory_tokens, 'memory_mask': memory_mask}
    _L0_xattn_all = _L0_xattn_setup()
    _L0_xattn_in = {k: v for k, v in _L0_xattn_all.items() if k in ()}
    del _L0_xattn_all

    def _L0_attn_setup():
        import jax, jax.numpy as jnp
        import numpy as np
        EMBED = 1024
        HEADS = 16
        NOPE = 128
        VDIM = 128
        ROPE = 64
        Q_HEAD = NOPE + ROPE
        KV_RANK = 256
        BASE = 10000.0

        def _rope(x, offset=0):
            d = x.shape[-1]
            n = x.shape[-2]
            theta = BASE ** (-2.0 * jnp.arange(d // 2, dtype=jnp.float32) / d)
            pos = jnp.arange(n, dtype=jnp.float32) + offset
            ang = pos[:, None] * theta[None, :]
            cos, sin = (jnp.cos(ang), jnp.sin(ang))
            x1 = x[..., 0::2]
            x2 = x[..., 1::2]
            o1 = x1 * cos - x2 * sin
            o2 = x1 * sin + x2 * cos
            return jnp.stack([o1, o2], axis=-1).reshape(x.shape)
        key = jax.random.key(seed)
        ks = jax.random.split(key, 6)
        b, n = (2, 1024)
        s = lambda fin: 1.0 / np.sqrt(fin)
        return {'x': jax.random.normal(ks[0], (b, n, EMBED), jnp.float32), 'Wqa': jax.random.normal(ks[1], (EMBED, 256), jnp.float32) * s(EMBED), 'Wqb': jax.random.normal(ks[2], (256, HEADS * Q_HEAD), jnp.float32) * s(256), 'Wkva': jax.random.normal(ks[3], (EMBED, KV_RANK + ROPE), jnp.float32) * s(EMBED), 'Wkvb': jax.random.normal(ks[4], (KV_RANK, HEADS * (NOPE + VDIM)), jnp.float32) * s(KV_RANK), 'Wout': jax.random.normal(ks[5], (HEADS * VDIM, EMBED), jnp.float32) * s(HEADS * VDIM)}
    _L0_attn_all = _L0_attn_setup()
    _L0_attn_in = {k: v for k, v in _L0_attn_all.items() if k in ('Wqa', 'Wqb', 'Wkva', 'Wkvb', 'Wout')}
    del _L0_attn_all

    def _L0_ffn_setup():
        import jax, jax.numpy as jnp
        import numpy as np
        from jax import lax
        DIM = 1024
        E = 8
        K = 2
        RANK = 32
        CAP_FACTOR = 1.25

        def gelu(x):
            return jax.nn.gelu(x, approximate=False)

        def _moe_forward(x, gate_w, w1, b1, w2, b2, wd, wu, sw1, sb1, sw2, sb2, swd, swu):
            B, S, D = x.shape
            T = B * S
            cap = max(1, int(T * CAP_FACTOR / E))
            xt = x.reshape(T, D)
            logits = xt @ gate_w
            probs_full = jax.nn.softmax(logits, axis=-1)
            top_p, top_i = lax.top_k(probs_full, K)
            out = jnp.zeros_like(xt)
            for k in range(K):
                e = top_i[:, k]
                w = top_p[:, k]
                onehot = jax.nn.one_hot(e, E, dtype=jnp.int32)
                pos_all = jnp.cumsum(onehot, axis=0) - 1
                pos = jnp.take_along_axis(pos_all, e[:, None], axis=1)[:, 0]
                keep = pos < cap
                pos_c = jnp.where(keep, pos, cap)
                buf = jnp.zeros((E, cap, D), x.dtype).at[e, pos_c].set(xt * keep[:, None].astype(x.dtype), mode='drop')
                h = gelu(jnp.einsum('ecd,edf->ecf', buf, w1) + b1[:, None, :])
                y = jnp.einsum('ecf,efd->ecd', h, w2) + b2[:, None, :]
                a = jnp.einsum('ecr,erd->ecd', gelu(jnp.einsum('ecd,edr->ecr', buf, wd)), wu)
                y = y + a
                tok = y[e, jnp.minimum(pos_c, cap - 1)]
                out = out + tok * keep[:, None].astype(x.dtype) * w[:, None]
            sh = gelu(xt @ sw1 + sb1) @ sw2 + sb2
            sh = sh + gelu(xt @ swd) @ swu
            out = out + 0.2 * sh
            return out.reshape(B, S, D)
        key = jax.random.key(seed)
        ks = jax.random.split(key, 16)
        s = 0.02
        d, h = (DIM, 4 * DIM)
        inp = {'x': jax.random.normal(ks[0], (4, 1024, d), dtype=jnp.float32), 'gate_w': jax.random.normal(ks[1], (d, E), dtype=jnp.float32) * s, 'w1': jax.random.normal(ks[2], (E, d, h), dtype=jnp.float32) * s, 'b1': jnp.zeros((E, h), dtype=jnp.float32), 'w2': jax.random.normal(ks[3], (E, h, d), dtype=jnp.float32) * s, 'b2': jnp.zeros((E, d), dtype=jnp.float32), 'wd': jax.random.normal(ks[4], (E, d, RANK), dtype=jnp.float32) * s, 'wu': jax.random.normal(ks[5], (E, RANK, d), dtype=jnp.float32) * s, 'sw1': jax.random.normal(ks[6], (d, h), dtype=jnp.float32) * s, 'sb1': jnp.zeros((h,), dtype=jnp.float32), 'sw2': jax.random.normal(ks[7], (h, d), dtype=jnp.float32) * s, 'sb2': jnp.zeros((d,), dtype=jnp.float32), 'swd': jax.random.normal(ks[8], (d, RANK), dtype=jnp.float32) * s, 'swu': jax.random.normal(ks[9], (RANK, d), dtype=jnp.float32) * s}
        return inp
    _L0_ffn_all = _L0_ffn_setup()
    _L0_ffn_in = {k: v for k, v in _L0_ffn_all.items() if k in ('gate_w', 'w1', 'b1', 'w2', 'b2', 'wd', 'wu', 'sw1', 'sb1', 'sw2', 'sb2', 'swd', 'swu')}
    del _L0_ffn_all
    return {'x': x, 'ctx_2048': ctx_2048, 'mask_BxS2_bk0': mask_BxS2_bk0, 'L0_attn_Wqa': _L0_attn_in['Wqa'], 'L0_attn_Wqb': _L0_attn_in['Wqb'], 'L0_attn_Wkva': _L0_attn_in['Wkva'], 'L0_attn_Wkvb': _L0_attn_in['Wkvb'], 'L0_attn_Wout': _L0_attn_in['Wout'], 'L0_ffn_gate_w': _L0_ffn_in['gate_w'], 'L0_ffn_w1': _L0_ffn_in['w1'], 'L0_ffn_b1': _L0_ffn_in['b1'], 'L0_ffn_w2': _L0_ffn_in['w2'], 'L0_ffn_b2': _L0_ffn_in['b2'], 'L0_ffn_wd': _L0_ffn_in['wd'], 'L0_ffn_wu': _L0_ffn_in['wu'], 'L0_ffn_sw1': _L0_ffn_in['sw1'], 'L0_ffn_sb1': _L0_ffn_in['sb1'], 'L0_ffn_sw2': _L0_ffn_in['sw2'], 'L0_ffn_sb2': _L0_ffn_in['sb2'], 'L0_ffn_swd': _L0_ffn_in['swd'], 'L0_ffn_swu': _L0_ffn_in['swu']}

def reference(x, ctx_2048, mask_BxS2_bk0, L0_attn_Wqa, L0_attn_Wqb, L0_attn_Wkva, L0_attn_Wkvb, L0_attn_Wout, L0_ffn_gate_w, L0_ffn_w1, L0_ffn_b1, L0_ffn_w2, L0_ffn_b2, L0_ffn_wd, L0_ffn_wu, L0_ffn_sw1, L0_ffn_sb1, L0_ffn_sw2, L0_ffn_sb2, L0_ffn_swd, L0_ffn_swu):
    import jax
    import jax.numpy as jnp

    def _L0_xattn_ref(hidden_states, memory_tokens, memory_mask):
        import jax, jax.numpy as jnp
        import numpy as np
        B, S, D = hidden_states.shape
        scale = 1.0 / jnp.sqrt(jnp.asarray(D, hidden_states.dtype))
        scores = jnp.einsum('bsd,bmd->bsm', hidden_states, memory_tokens) * scale
        neg_inf = jnp.asarray(-1e+30, scores.dtype)
        scores = jnp.where(memory_mask[:, None, :], scores, neg_inf)
        attn = jax.nn.softmax(scores, axis=-1)
        readout = jnp.einsum('bsm,bmd->bsd', attn, memory_tokens)
        valid_b = jnp.any(memory_mask, axis=-1)
        out = jnp.where(valid_b[:, None, None], readout, jnp.zeros_like(readout))
        return out

    def _L0_attn_ref(x, Wqa, Wqb, Wkva, Wkvb, Wout):
        import jax, jax.numpy as jnp
        import numpy as np
        EMBED = 1024
        HEADS = 16
        NOPE = 128
        VDIM = 128
        ROPE = 64
        Q_HEAD = NOPE + ROPE
        KV_RANK = 256
        BASE = 10000.0

        def _rope(x, offset=0):
            d = x.shape[-1]
            n = x.shape[-2]
            theta = BASE ** (-2.0 * jnp.arange(d // 2, dtype=jnp.float32) / d)
            pos = jnp.arange(n, dtype=jnp.float32) + offset
            ang = pos[:, None] * theta[None, :]
            cos, sin = (jnp.cos(ang), jnp.sin(ang))
            x1 = x[..., 0::2]
            x2 = x[..., 1::2]
            o1 = x1 * cos - x2 * sin
            o2 = x1 * sin + x2 * cos
            return jnp.stack([o1, o2], axis=-1).reshape(x.shape)
        b, n, _ = x.shape
        q = x @ Wqa @ Wqb
        q = q.reshape(b, n, HEADS, Q_HEAD).transpose(0, 2, 1, 3)
        q_nope, q_pe = (q[..., :NOPE], q[..., NOPE:])
        ckv = x @ Wkva
        compressed, k_pe = (ckv[..., :KV_RANK], ckv[..., KV_RANK:])
        k_pe = jnp.broadcast_to(k_pe[:, None], (b, HEADS, n, ROPE))
        kv = compressed @ Wkvb
        kv = kv.reshape(b, n, HEADS, NOPE + VDIM).transpose(0, 2, 1, 3)
        k_nope, v = (kv[..., :NOPE], kv[..., NOPE:])
        q_pe = _rope(q_pe)
        k_pe = _rope(k_pe)
        qf = jnp.concatenate([q_nope, q_pe], axis=-1)
        kf = jnp.concatenate([k_nope, k_pe], axis=-1)
        scale = 1.0 / np.sqrt(Q_HEAD)
        scores = jnp.einsum('bhnd,bhmd->bhnm', qf, kf) * scale
        causal = jnp.tril(jnp.ones((n, n), dtype=bool))
        scores = jnp.where(causal, scores, jnp.finfo(scores.dtype).min)
        attn = jax.nn.softmax(scores, axis=-1)
        out = jnp.einsum('bhnm,bhmd->bhnd', attn, v)
        out = out.transpose(0, 2, 1, 3).reshape(b, n, HEADS * VDIM)
        return out @ Wout

    def _L0_ffn_ref(x, gate_w, w1, b1, w2, b2, wd, wu, sw1, sb1, sw2, sb2, swd, swu):
        import jax, jax.numpy as jnp
        import numpy as np
        from jax import lax
        DIM = 1024
        E = 8
        K = 2
        RANK = 32
        CAP_FACTOR = 1.25

        def gelu(x):
            return jax.nn.gelu(x, approximate=False)

        def _moe_forward(x, gate_w, w1, b1, w2, b2, wd, wu, sw1, sb1, sw2, sb2, swd, swu):
            B, S, D = x.shape
            T = B * S
            cap = max(1, int(T * CAP_FACTOR / E))
            xt = x.reshape(T, D)
            logits = xt @ gate_w
            probs_full = jax.nn.softmax(logits, axis=-1)
            top_p, top_i = lax.top_k(probs_full, K)
            out = jnp.zeros_like(xt)
            for k in range(K):
                e = top_i[:, k]
                w = top_p[:, k]
                onehot = jax.nn.one_hot(e, E, dtype=jnp.int32)
                pos_all = jnp.cumsum(onehot, axis=0) - 1
                pos = jnp.take_along_axis(pos_all, e[:, None], axis=1)[:, 0]
                keep = pos < cap
                pos_c = jnp.where(keep, pos, cap)
                buf = jnp.zeros((E, cap, D), x.dtype).at[e, pos_c].set(xt * keep[:, None].astype(x.dtype), mode='drop')
                h = gelu(jnp.einsum('ecd,edf->ecf', buf, w1) + b1[:, None, :])
                y = jnp.einsum('ecf,efd->ecd', h, w2) + b2[:, None, :]
                a = jnp.einsum('ecr,erd->ecd', gelu(jnp.einsum('ecd,edr->ecr', buf, wd)), wu)
                y = y + a
                tok = y[e, jnp.minimum(pos_c, cap - 1)]
                out = out + tok * keep[:, None].astype(x.dtype) * w[:, None]
            sh = gelu(xt @ sw1 + sb1) @ sw2 + sb2
            sh = sh + gelu(xt @ swd) @ swu
            out = out + 0.2 * sh
            return out.reshape(B, S, D)
        return _moe_forward(x, gate_w, w1, b1, w2, b2, wd, wu, sw1, sb1, sw2, sb2, swd, swu)
    x = x + _L0_xattn_ref(_layernorm(x, axis=-1), ctx_2048, mask_BxS2_bk0)
    x = x + _L0_attn_ref(_layernorm(x, axis=-1), L0_attn_Wqa, L0_attn_Wqb, L0_attn_Wkva, L0_attn_Wkvb, L0_attn_Wout)
    x = x + _L0_ffn_ref(_layernorm(x, axis=-1), L0_ffn_gate_w, L0_ffn_w1, L0_ffn_b1, L0_ffn_w2, L0_ffn_b2, L0_ffn_wd, L0_ffn_wu, L0_ffn_sw1, L0_ffn_sb1, L0_ffn_sw2, L0_ffn_sb2, L0_ffn_swd, L0_ffn_swu)
    return x

_drawn_inputs = setup_inputs


def setup_inputs(seed=0):
    import zlib

    import numpy as np

    out = dict(_drawn_inputs(seed))
    spreads = {'L0_ffn_b1': (0.0, 0.424),
     'L0_ffn_b2': (0.0, 0.349),
     'L0_ffn_sb1': (0.0, 0.637),
     'L0_ffn_sb2': (0.0, 0.503)}
    factors = {'L0_ffn_wd': 6.195, 'L0_ffn_wu': 5.935, 'L0_ffn_swd': 8.0, 'L0_ffn_swu': 8.0}
    for name, (base, spread) in spreads.items():
        noise = np.random.default_rng([zlib.crc32(name.encode()), seed]).standard_normal(out[name].shape)
        drawn = base * np.exp(spread * noise) if base else spread * noise
        out[name] = jnp.asarray(drawn.astype(out[name].dtype))
    for name, factor in factors.items():
        out[name] = (out[name] * factor).astype(out[name].dtype)
    return out
```

```python
from contextlib import ExitStack

import concourse.bass as bass
from concourse import mybir

F32 = mybir.dt.float32
F32R = mybir.dt.float32r
BF16 = mybir.dt.bfloat16
I32 = mybir.dt.int32
U32 = mybir.dt.uint32
U8 = mybir.dt.uint8
ALU = mybir.AluOpType
ACT = mybir.ActivationFunctionType
X = mybir.AxisListType.X

P = 128
D = 1024
TOK = 256
NT = TOK // P
NC = D // P
HALF = 512
KEYS = 25088
NBLK = KEYS // HALF
KJ = HALF // P
NLIST = 56
H = 16
NOPE = 128
ROPE = 64
QH = NOPE + ROPE
RANK = 256
NR = RANK // P
E = 8
TOPK = 2
CAP = int(TOK * 1.25 / E)
SLOTS = TOPK * CAP
F = 4096
NF = F // P
AR = 32
TILE = 4096
HT = TILE // 2
STEPS = F // HALF
RAW = 6
SPLIT = 3
ROUND = [("w1", 0)] + [x for k in range(1, STEPS) for x in (("w1", k), ("w2", k - 1))]\
    + [("s1", 0), ("w2", STEPS - 1), ("s2", 0)]
NHALF = 2 * len(ROUND)
assert NHALF % RAW == 0 and NHALF % SPLIT == 0
FIRST_HALF = {tile: 2 * n for n, tile in enumerate(ROUND)}
NEG = -1e30
SCALE = QH ** -0.5
EPS = 1e-5

C_ID, C_UP, C_CAUS = 0, 128, 256
C_COS, C_SIN = 384, 448
C_I8, C_I40, C_BNO = 512, 520, 560
NCONST = 560 + NBLK


def build(nc, x, ctx, mask, Wqa, Wqb, Wkva, Wkvb, Wout, gate_w, w1, b1, w2, b2, wd, wu,
          sw1, sb1, sw2, sb2, swd, swu, consts, out):
    with ExitStack() as stack:
        def sb(name, shape, dt=F32):
            return stack.enter_context(nc.sbuf_tensor(name, shape, dt))

        def sem(name):
            return stack.enter_context(nc.semaphore(name))

        x_sb = sb("x_sb", [P, NT, D])
        cst = sb("cst", [P, NCONST])
        ident = cst[:, C_ID:C_ID + P]
        cos = cst[:, C_COS:C_COS + NT * 32].rearrange("p (t i) -> p t i", t=NT)
        sin = cst[:, C_SIN:C_SIN + NT * 32].rearrange("p (t i) -> p t i", t=NT)
        identb = sb("identb", [P, P], BF16)
        upperb = sb("upperb", [P, P], BF16)
        causalb = sb("causalb", [P, P], BF16)
        onesb = sb("onesb", [P, P], BF16)
        onesf = sb("onesf", [P, P])
        gate_sb = sb("gate_sb", [P, NC, E])
        b1T = sb("b1T", [P, (E + 1) * NF])
        ln_st = sb("ln_st", [P, NT, 2, 6])
        ln_mv = sb("ln_mv", [P, NT, 2])
        ln_var = sb("ln_var", [P, NT])
        ln_sd = sb("ln_sd", [P, NT])
        ln_rs = sb("ln_rs", [P, NT])
        mask_blocks = sb("mask_blocks", [NBLK, HALF], U8)
        any_blk = sb("any_blk", [NBLK, 1])
        work = sb("work", [1, NLIST])
        work2 = sb("work2", [1, NLIST])
        order = sb("order", [1, NLIST])
        pair_on = sb("pair_on", [1, NLIST // 2])
        pairs_f = sb("pairs_f", [1, 1])
        order_c = sb("order_c", [1, NLIST])
        mask_ix = sb("mask_ix", [1, NLIST], I32)
        ctx_ix = sb("ctx_ix", [1, NLIST], I32)
        pairs_i = sb("pairs_i", [1, 1], I32)
        valid = sb("valid", [P, 1])
        run_max = sb("run_max", [P, NT])
        blk_max = sb("blk_max", [P, NT])
        new_max = sb("new_max", [P, NT])
        neg_max = sb("neg_max", [P, NT])
        old_less_new = sb("old_less_new", [P, NT])
        alpha = sb("alpha", [P, NT])
        row_sum = sb("row_sum", [P, NT])
        run_sum = sb("run_sum", [P, NT])
        inv_sum = sb("inv_sum", [P, NT])
        inv_valid = sb("inv_valid", [P, NT])
        s_max = sb("s_max", [P, 2, NT])
        s_bias = sb("s_bias", [P, 2, NT])
        s_sum = sb("s_sum", [P, 2, NT])
        s_inv = sb("s_inv", [P, 2, NT])
        b1_e = sb("b1_e", [P, NF + 4])
        g_max = sb("g_max", [P, NT])
        g_neg = sb("g_neg", [P, NT])
        g_exp = sb("g_exp", [P, NT, E])
        g_sum = sb("g_sum", [P, NT])
        g_inv = sb("g_inv", [P, NT])
        probs = sb("probs", [P, NT, E])
        top_v = sb("top_v", [P, NT, 8])
        top_i = sb("top_i", [P, NT, 8], U32)
        top_f = sb("top_f", [P, NT, 8])
        onehot = sb("onehot", [P, NT, E, TOPK])
        onehotb = sb("onehotb", [P, NT, E * TOPK], BF16)
        far = sb("far", [P, NT, E * TOPK])
        slot = sb("slot", [P, NT, E * TOPK])
        early = ExitStack()

        def sb_early(name, shape, dt=F32):
            return early.enter_context(nc.sbuf_tensor(name, shape, dt))

        ring = sb_early("ring", [P, 8, TILE])
        h = sb_early("h", [P, 2 * NT * D])
        hN = h[:, 0:NT * D].rearrange("p (t d) -> p t d", t=NT)
        hT = h[:, NT * D:2 * NT * D].rearrange("p (c t) -> p c t", c=NC)
        attnT = h[:, :].rearrange("p (h t) -> p h t", h=H)
        arena = sb_early("arena", [P, 11520])

        def part_of(memory):
            def part(at, shape, rows=P):
                n = 1
                for s in shape:
                    n *= s
                v = memory[0:rows, at:at + n]
                if len(shape) == 2:
                    return v.rearrange("p (a b) -> p a b", a=shape[0])
                if len(shape) == 3:
                    return v.rearrange("p (a b c) -> p a b c", a=shape[0], b=shape[1])
                return v
            return part

        part = part_of(arena)

        o_acc = part(0, [NT, D])
        prob = part(2048, [NT, 2 * HALF])
        probT = part(4096, [NT, 2 * KJ * P])
        b1_raw = part(9728, [3, P])
        mask_row = arena[0:1, 6144:6400].bitcast(U8).rearrange("p (b n) -> p b n", b=2)
        bias_row = arena[0:1, 6400:6912].bitcast(BF16).rearrange("p (b n) -> p b n", b=2)
        kT = [ring[:, 2 + b, :].rearrange("p (c k) -> p c k", c=NC) for b in range(2)]
        ctx_t = [ring[:, b, :].rearrange("p (j d) -> p j d", j=KJ) for b in range(2)]

        tail4 = ring[:, 4:8, :].rearrange("p s n -> p (s n)")
        wqb_sb = tail4[:, 0:6144].rearrange("p (k h n) -> p k h n", k=NR, h=H)
        wkvb_sb = tail4[:, 6144:14336].rearrange("p (k h n) -> p k h n", k=NR, h=H)
        wqa_sb = tail4[:, 14336:16384].rearrange("p (c n) -> p c n", c=NC)
        wkva_sb = part(7168, [NC, RANK + ROPE])
        wout_sb = ring[:, 0:4, :].rearrange("p s (h n) -> p (s h) n", h=4)
        qaT = part(0, [NR, TOK])
        compT = part(512, [NR, TOK])
        q_rot = part(1024, [H, ROPE])
        rope_tmp = part(2048, [4, 256])
        q_peT = part(3072, [H // 2, TOK])
        k_rot = part(5120, [NT, 2, ROPE])
        k_peT = part(5376, [TOK])
        qkT = part(5632, [2, 2 * TOK])
        v_sb = part(7168, [NT, H, NOPE])
        p_sb = part(1024, [2, 3, P])
        pT_sb = part(2048, [2, 3, P])


        early.close()
        hN_s = [sb(f"hN_{n}", [P, NT, D], F32R) for n in ("hi", "lo")]
        hT_s = [sb(f"hT_{n}", [P, NC, TOK], F32R) for n in ("hi", "lo")]
        w_s = [sb(f"w_{n}", [P, SPLIT, HT], F32R) for n in ("hi", "lo")]
        raw = sb("raw", [P, RAW, HT])
        sel = sb("sel", [P, NT, (E + 1) * SLOTS], F32R)
        xs_s = [sb(f"xs_{n}", [P, NC, SLOTS], F32R) for n in ("hi", "lo")]
        hid_s = [sb(f"hid_{n}", [P, 2, 4, SLOTS], F32R) for n in ("hi", "lo")]
        shid_s = [sb(f"shid_{n}", [P, 4, TOK], F32R) for n in ("hi", "lo")]
        late = sb("late", [P, 8208])
        late_part = part_of(late)
        fN = late_part(0, [NT, D])
        a_sb = late_part(0, [HALF], rows=SLOTS)
        y_sb = late_part(1024, [2, HALF], rows=SLOTS)
        fT = late_part(2048, [NC, TOK])
        combT = late_part(2048, [E, TOK], rows=SLOTS)
        selw = late_part(4096, [NT, E * SLOTS])
        shid = late_part(4096, [4, TOK])
        xs = late_part(5376, [NC, SLOTS])
        hid = late_part(6016, [4, SLOTS])
        wd_sb = late_part(6336, [NC, AR])
        wub_sb = late_part(6592, [2, HALF], rows=AR + 1)
        ga = late_part(7616, [SLOTS], rows=AR + 1)
        gs = late_part(7696, [TOK], rows=AR + 1)
        ct_e = late_part(7952, [TOK], rows=SLOTS)
        ps = stack.enter_context(nc.psum_tensor("ps", [P, 8, HALF], F32))

        consts_in, x_in, mask_in, small_in = sem("consts_in"), sem("x_in"), sem("mask_in"), sem("small_in")
        dve_chain = sem("dve_chain")
        ones_set, constb_set = sem("ones_set"), sem("constb_set")
        any_ready, any_ps, list_ready = sem("any_ready"), sem("any_ps"), sem("list_ready")
        b1_ps, b1T_ready = sem("b1_ps"), sem("b1T_ready")
        ln_var_ready = [sem(f"ln_var_ready{n}") for n in range(3)]
        ln_sd_ready = [sem(f"ln_sd_ready{n}") for n in range(3)]
        ln_h_ready = [sem(f"ln_h_ready{n}") for n in range(3)]
        lnT_ps = [sem(f"lnT_ps{n}") for n in range(3)]
        lnT_act = [sem(f"lnT_act{n}") for n in range(3)]
        lnT_dve = [sem(f"lnT_dve{n}") for n in range(3)]
        ctx_in = [sem(f"ctx_in{b}") for b in range(2)]
        mrow_in = [sem(f"mrow_in{b}") for b in range(2)]
        bias_ready = sem("bias_ready")
        pair_done = sem("pair_done")
        t_filled = [sem(f"t_filled{b}") for b in range(2)]
        t_drained = [sem(f"t_drained{b}") for b in range(2)]
        s_ready = [sem(f"s_ready{q}") for q in range(NT)]
        blk_max_ready = [sem(f"blk_max_ready{q}") for q in range(NT)]
        new_max_ready = [sem(f"new_max_ready{q}") for q in range(NT)]
        exp_args_ready = [sem(f"exp_args_ready{q}") for q in range(NT)]
        p_ready = [sem(f"p_ready{q}") for q in range(NT)]
        pv_ready = [sem(f"pv_ready{q}") for q in range(NT)]
        o_added = [sem(f"o_added{q}") for q in range(NT)]
        wq_in, wkv_in, wout_in = sem("wq_in"), sem("wkv_in"), [sem(f"wout_in{s}") for s in range(4)]
        proj_ps, qaT_ready, compT_ready = sem("proj_ps"), sem("qaT_ready"), sem("compT_ready")
        kpe_ps, k_rot_ready, kpeT_ps, kpeT_ready = sem("kpe_ps"), sem("k_rot_ready"), sem("kpeT_ps"), sem("kpeT_ready")
        qpe_ps, q_rot_ready, qpeT_ps, qpeT_ready = sem("qpe_ps"), sem("q_rot_ready"), sem("qpeT_ps"), sem("qpeT_ready")
        v_ps, v_ready = sem("v_ps"), sem("v_ready")
        qk_ps, qk_ready = sem("qk_ps"), sem("qk_ready")
        hs_ps, hmax_ready, hexp_ready, hp_ready = sem("hs_ps"), sem("hmax_ready"), sem("hexp_ready"), sem("hp_ready")
        pT_ps, pT_ready = sem("pT_ps"), sem("pT_ready")
        ho_ps, ho_ready = sem("ho_ps"), sem("ho_ready")
        wout_used = sem("wout_used")
        x2_ready = sem("x2_ready")
        gate_ps, g_neg_ready, g_exp_ready = sem("gate_ps"), sem("g_neg_ready"), sem("g_exp_ready")
        onehot_ready, pos_ps, sel_ready = sem("onehot_ready"), sem("pos_ps"), sem("sel_ready")
        combT_ps, combT_ready = sem("combT_ps"), sem("combT_ready")
        gate_in, swd_used = sem("gate_in"), sem("swd_used")
        norm_hi, norm_lo = sem("norm_hi"), sem("norm_lo")
        raw_in = [sem(f"raw_in{s}") for s in range(RAW)]
        w_hi_done, w_lo_done, w_used = sem("w_hi_done"), sem("w_lo_done"), sem("w_used")
        wd_in, wub_in = sem("wd_in"), sem("wub_in")
        gather_ps, xs_hi_done, xs_ready = sem("gather_ps"), sem("xs_hi_done"), sem("xs_ready")
        adapt_ps, ga_ready, gs_ready = sem("adapt_ps"), sem("ga_ready"), sem("gs_ready")
        a_copied, a_turned = sem("a_copied"), sem("a_turned")
        gelu_done, b1e_ready = sem("gelu_done"), sem("b1e_ready")
        hid_hi_done, hid_ready = sem("hid_hi_done"), sem("hid_ready")
        sgelu_done, shid_hi_done, shid_ready = sem("sgelu_done"), sem("shid_hi_done"), sem("shid_ready")
        y_ps, y_ready, ct_ready = sem("y_ps"), sem("y_ready"), sem("ct_ready")
        comb_ps, comb_added, sh_added = sem("comb_ps"), sem("comb_added"), sem("sh_added")
        sh_ps, out_ready, out_stored = sem("sh_ps"), sem("out_ready"), sem("out_stored")

        ctx_v = ctx.rearrange("(b p j) d -> b p j d", p=P, j=KJ)
        mask_rows_v = mask.rearrange("(b n) -> b n", n=HALF)
        out_v = out.rearrange("a (t p) d -> p (a t) d", p=P)

        def half_source(e, n):
            (kind, k), x = ROUND[n // 2], n % 2
            if kind == "w1":
                return w1[bass.ds(e, 1)].rearrange("a (c p) f -> p (a c) f", p=P)[:, 4 * x:4 * x + 4, k * HALF:(k + 1) * HALF]
            if kind == "w2":
                return w2[bass.ds(e, 1)].rearrange("a (k x j p) d -> k x p (a j) d", x=2, j=2, p=P)[k, x]
            if kind == "s1":
                return sw1.rearrange("(c p) (s x f) -> s x p c f", p=P, s=STEPS, x=2)[bass.ds(e, 1), x]\
                    .rearrange("a p c f -> (a p) c f")
            return sw2.rearrange("(s x j p) d -> s x p j d", x=2, j=2, p=P)[bass.ds(e, 1), x].rearrange("a p j d -> (a p) j d")

        def half_view(v, n):
            return v.rearrange("p (c f) -> p c f", c={"w1": 4, "w2": 2, "s1": 8, "s2": 2}[ROUND[n // 2][0]])

        out_sb = late_part(4096, [NT, D])
        block = stack.enter_context(nc.Block())

        @block.sync
        def _(sp):
            sp.dma_start(mask_blocks[:, :], mask_rows_v[1:1 + NBLK, :]).then_inc(mask_in, 16)
            sp.dma_start(cst[:, :], consts).then_inc(consts_in, 16)
            sp.dma_start(x_sb[:, :, :], x.rearrange("a (t p) d -> p (a t) d", p=P)).then_inc(x_in, 16)
            sp.dma_start(b1_raw[:, 0:2, :], b1.rearrange("e (f q) -> (e f) q", q=P).rearrange("(a r) q -> r a q", r=P))\
                .then_inc(small_in, 16)
            sp.dma_start(b1_raw[0:NF, 2, :], sb1.rearrange("(f q) -> f q", q=P)).then_inc(small_in, 16)
            sp.wait_ge(list_ready, 1)
            pairs = sp.value_load(pairs_i[0:1, 0:1], min_val=1, max_val=NLIST // 2)
            with sp.Fori(0, pairs) as i:
                sp.wait_ge(pair_done, i + 1)
                for b in range(2):
                    c = sp.value_load(ctx_ix[0:1, bass.ds(i * 2 + b, 1)], min_val=0, max_val=NBLK - 1)
                    m = sp.value_load(mask_ix[0:1, bass.ds(i * 2 + b, 1)], min_val=0, max_val=NBLK)
                    sp.dma_start(mask_row[0:1, b, :], mask_rows_v[bass.ds(m, 1), :]).then_inc(mrow_in[b], 16)
                    sp.dma_start(ctx_t[b], ctx_v[bass.ds(c, 1)].rearrange("b p j d -> (b p) j d")).then_inc(ctx_in[b], 16)
            sp.dma_start(wqa_sb, Wqa.rearrange("(c p) n -> p c n", p=P)).then_inc(wq_in, 16)
            sp.dma_start(wkva_sb, Wkva.rearrange("(c p) n -> p c n", p=P)).then_inc(wkv_in, 16)
            sp.dma_start(wqb_sb.rearrange("p k h n -> p k (h n)"),
                         Wqb.rearrange("(k p) n -> p k n", p=P)).then_inc(wq_in, 16)
            sp.dma_start(wkvb_sb.rearrange("p k h n -> p k (h n)"),
                         Wkvb.rearrange("(k p) n -> p k n", p=P)).then_inc(wkv_in, 16)
            sp.dma_start(gate_sb[:, :, :], gate_w.rearrange("(c p) e -> p c e", p=P)).then_inc(gate_in, 16)
            sp.wait_ge(ln_h_ready[1], 1)
            for s in range(4):
                sp.dma_start(wout_sb[:, 4 * s:4 * s + 4, :],
                             Wout[s * HALF:(s + 1) * HALF, :].rearrange("(h p) n -> p h n", p=P)).then_inc(wout_in[s], 16)
            sp.wait_ge(qk_ps, H)
            for n in range(RAW):
                sp.dma_start(half_view(raw[:, n, :], n), half_source(0, n)).then_inc(raw_in[n], 16)
            sp.wait_ge(x2_ready, NT * 2)
            sp.dma_start(wd_sb, swd.rearrange("(c p) r -> p c r", p=P)).then_inc(wd_in, 16)
            sp.dma_start(wub_sb[0:AR].rearrange("p a b -> p (a b)"), wu[0]).then_inc(wub_in, 16)
            sp.dma_start(wub_sb[AR:AR + 1].rearrange("p a b -> p (a b)"), b2[0:1, :]).then_inc(wub_in, 16)
            sp.wait_ge(adapt_ps, 1)
            sp.dma_start(wd_sb, wd[0].rearrange("(c p) r -> p c r", p=P)).then_inc(wd_in, 16)

            def load(e, n, source_e, m):
                sp.wait_ge(w_lo_done, NHALF * e + n + 1)
                sp.dma_start(half_view(raw[:, m % RAW, :], m), half_source(source_e, m)).then_inc(raw_in[m % RAW], 16)

            with sp.Fori(0, E - 1) as e:
                for n in range(NHALF):
                    if n + RAW < NHALF:
                        load(e, n, e, n + RAW)
                    else:
                        load(e, n, e + 1, n + RAW - NHALF)
                    if n == 6:
                        sp.wait_ge(adapt_ps, e + 2)
                        sp.dma_start(wd_sb, wd[bass.ds(e + 1, 1)].rearrange("a (c p) r -> p (a c) r", p=P)).then_inc(wd_in, 16)
                sp.wait_ge(y_ps, e + 1)
                sp.dma_start(wub_sb[0:AR].rearrange("p a b -> p (a b)"),
                             wu[bass.ds(e + 1, 1)].rearrange("a r d -> (a r) d")).then_inc(wub_in, 16)
                sp.dma_start(wub_sb[AR:AR + 1].rearrange("p a b -> p (a b)"), b2[bass.ds(e + 1, 1), :])\
                    .then_inc(wub_in, 16)
            for n in range(NHALF - RAW):
                load(E - 1, n, E - 1, n + RAW)
            sp.wait_ge(y_ps, E)
            sp.dma_start(wub_sb[0:AR].rearrange("p a b -> p (a b)"), swu).then_inc(wub_in, 16)
            sp.dma_start(wub_sb[AR:AR + 1].rearrange("p a b -> p (a b)"), sb2.rearrange("(a d) -> a d", a=1))\
                .then_inc(wub_in, 16)
            for t in range(NT):
                for a in range(2):
                    sp.wait_ge(out_ready, 2 * t + a + 1)
                    sp.dma_start(out_v[:, t, a * HALF:(a + 1) * HALF], out_sb[:, t, a * HALF:(a + 1) * HALF])\
                        .then_inc(out_stored, 16)
            sp.wait_ge(out_stored, 16 * NT * 2)

        @block.scalar
        def _(act):
            def layernorm_sd(n):
                act.wait_ge(ln_var_ready[n], 1)
                nc.scalar.activation(ln_sd[:, :], ln_var[:, :], ACT.Sqrt).then_inc(ln_sd_ready[n], 1)

            def layernorm_drain(n, scale, hT=hT):
                for t in range(NT):
                    act.wait_ge(lnT_ps[n], 2 * t + 1)
                    nc.scalar.activation(hT[:, 0:4, t * P:(t + 1) * P], ps[:, 2 * t, :].rearrange("p (c q) -> p c q", c=4),
                                         ACT.Copy, scale=scale).then_inc(lnT_act[n], 1)

            act.sem_inc(t_drained[0], 1)
            layernorm_sd(0)
            layernorm_drain(0, 1.0 / 32)
            act.wait_ge(b1_ps, 1)
            nc.scalar.activation(b1T[:, :], ps[:, 7, 0:(E + 1) * NF], ACT.Copy).then_inc(b1T_ready, 1)

            act.wait_ge(list_ready, 1)
            pairs = act.value_load(pairs_i[0:1, 0:1], min_val=1, max_val=NLIST // 2)
            with act.Fori(0, pairs) as i:
                for b in range(2):
                    for c in range(0, NC, 2):
                        act.wait_ge(t_filled[0], 10 * i + 4 * b + c // 2 + 1)
                        nc.scalar.activation(kT[b][:, c, :], ps[:, 4, :], ACT.Copy).then_inc(t_drained[0], 1)
                for q in range(NT):
                    act.wait_ge(exp_args_ready[q], 2 * i + 2)
                    nc.scalar.activation(alpha[:, q:q + 1], old_less_new[:, q:q + 1], ACT.Exp)
                    nc.scalar.activation(prob[:, q, :].rearrange("p (b k) -> p b k", b=2), ps[:, 2 * q:2 * q + 2, :], ACT.Exp,
                                         bias=neg_max[:, q:q + 1], accum_out=row_sum[:, q:q + 1]).then_inc(p_ready[q], 1)
                    act.wait_ge(t_filled[0], 10 * i + 8 + q + 1)
                    nc.scalar.activation(probT[:, q, 0:HALF], ps[:, 4, :], ACT.Copy).then_inc(t_drained[0], 1)

            layernorm_sd(1)
            layernorm_drain(1, 1.0)
            act.wait_ge(proj_ps, 1)
            nc.scalar.activation(qaT, ps[:, 4, :].rearrange("p (k t) -> p k t", k=NR), ACT.Copy).then_inc(qaT_ready, 1)
            for n in range(2 * NT * 2):
                act.wait_ge(v_ps, n + 1)
                nc.scalar.activation(v_sb[:, n // 4, 4 * (n % 4):4 * (n % 4) + 4, :],
                                     ps[:, 4 + n % 2, :].rearrange("p (h v) -> p h v", h=4), ACT.Copy).then_inc(v_ready, 1)
            act.wait_ge(kpeT_ps, 1)
            nc.scalar.activation(k_peT, ps[:, 7, 0:TOK], ACT.Copy).then_inc(kpeT_ready, 1)
            for t in range(NT):
                act.wait_ge(qpeT_ps, t + 1)
                nc.scalar.activation(q_peT[:, :, t * P:(t + 1) * P],
                                     ps[:, 2 * t:2 * t + 2, :].rearrange("p b (h q) -> p (b h) q", h=4), ACT.Copy)\
                    .then_inc(qpeT_ready, 1)
            for s in range(H + 4):
                if s < H:
                    act.wait_ge(qk_ps, s + 1)
                    nc.scalar.activation(qkT[:, s % 2, :], ps[:, 4, :], ACT.Copy).then_inc(qk_ready, 1)
                if 0 <= s - 1 < H:
                    g = s - 1
                    act.wait_ge(hmax_ready, g + 1)
                    nc.scalar.activation(p_sb[:, g % 2, 0, :], ps[:, 5, 0:P], ACT.Exp, bias=s_bias[:, g % 2, 0:1],
                                         scale=SCALE, accum_out=s_sum[:, g % 2, 0:1])
                    nc.scalar.activation(p_sb[:, g % 2, 1:3, :], ps[:, 5, P:3 * P].rearrange("p (a k) -> p a k", a=2), ACT.Exp,
                                         bias=s_bias[:, g % 2, 1:2], scale=SCALE, accum_out=s_sum[:, g % 2, 1:2])\
                        .then_inc(hexp_ready, 1)
                if 0 <= s - 3 < H:
                    g = s - 3
                    act.wait_ge(ho_ps, g + 1)
                    nc.scalar.activation(attnT[:, g, :], ps[:, 7, 0:TOK], ACT.Copy).then_inc(ho_ready, 1)

            layernorm_sd(2)
            for t in range(NT):
                act.wait_ge(ln_h_ready[2], t + 1)
                nc.scalar.activation(hN_s[0][:, t, :], fN[:, t, :], ACT.Copy).then_inc(norm_hi, 1)
            layernorm_drain(2, 1.0, fT)
            act.wait_ge(g_neg_ready, 1)
            for t in range(NT):
                nc.scalar.activation(g_exp[:, t, :], ps[:, 4, t * E:(t + 1) * E], ACT.Exp, bias=g_neg[:, t:t + 1],
                                     accum_out=g_sum[:, t:t + 1]).then_inc(g_exp_ready, 1)
            act.wait_ge(lnT_act[2], NT)
            act.wait_ge(lnT_dve[2], NT)
            for t in range(NT):
                nc.scalar.activation(hT_s[0][:, :, t * P:(t + 1) * P], fT[:, :, t * P:(t + 1) * P], ACT.Copy)\
                    .then_inc(norm_hi, 1)
            act.wait_ge(adapt_ps, 1)
            nc.scalar.activation(gs[0:AR, :], ps[0:AR, 7, 0:TOK], ACT.Gelu).then_inc(gs_ready, 1)
            act.wait_ge(norm_lo, 2 * NT)
            for n in range(4):
                bank = (4, 5, 6, 3)[n]
                act.wait_ge(combT_ps, n + 1)
                nc.scalar.activation(combT[:, 2 * n:2 * n + 2, :],
                                     ps[0:SLOTS, bank, :].rearrange("p (e t) -> p e t", e=2), ACT.Copy).then_inc(combT_ready, 1)

            def gathered_hi(count):
                act.wait_ge(gather_ps, count)
                nc.scalar.activation(xs_s[0][:, :, :].rearrange("p (a c) s -> p a (c s)", a=2), ps[:, 0:2, 0:4 * SLOTS],
                                     ACT.Copy).then_inc(xs_hi_done, 1)
                nc.scalar.activation(xs.rearrange("p (a c) s -> p a (c s)", a=2), ps[:, 0:2, 0:4 * SLOTS], ACT.Copy)\
                    .then_inc(xs_hi_done, 1)

            act.sem_inc(sgelu_done, 1)
            gathered_hi(1)
            with act.Fori(0, E) as e:
                for n in range(NHALF):
                    at = NHALF * e + n
                    act.wait_ge(raw_in[n % RAW], 16 * (NHALF // RAW * e + n // RAW + 1))
                    act.wait_ge(w_used, at + 1)
                    nc.scalar.activation(w_s[0][:, n % SPLIT, :], raw[:, n % RAW, :], ACT.Copy).then_inc(w_hi_done, 1)
                    if n == 2:
                        act.wait_ge(adapt_ps, e + 2)
                        nc.scalar.activation(ga[0:AR, :], ps[0:AR, 7, 0:SLOTS], ACT.Gelu).then_inc(ga_ready, 1)
                    for k in range(STEPS):
                        first = FIRST_HALF["w1", k]
                        if n == first + 3:
                            act.wait_ge(w_used, NHALF * e + first + 2 + SPLIT)
                            nc.scalar.activation(a_sb, ps[0:SLOTS, k % 2, :], ACT.Copy).then_inc(a_copied, 1)
                        if n == first + 4:
                            act.wait_ge(a_turned, STEPS * e + k + 1)
                            if k == 0:
                                act.wait_ge(b1e_ready, e + 1)
                            for j in range(4):
                                last = nc.scalar.activation(hid[:, j, :], ps[:, 2, j * SLOTS:(j + 1) * SLOTS], ACT.Gelu,
                                                            bias=b1_e[:, 4 * k + j:4 * k + j + 1])
                            last.then_inc(gelu_done, 1)
                    if n == FIRST_HALF["s1", 0] + 3:
                        act.wait_ge(w_used, NHALF * e + FIRST_HALF["s1", 0] + 2 + SPLIT)
                        for j in range(4):
                            last = nc.scalar.activation(shid[:, j, :], ps[:, 5 + j // 2, (j % 2) * TOK:(j % 2 + 1) * TOK],
                                                        ACT.Gelu, bias=b1_e[:, NF + j:NF + j + 1])
                        last.then_inc(sgelu_done, 1)
                        gathered_hi(e + 2)

        @block.vector
        def _(dve):
            chain = [0]

            def link(ins):
                chain[0] += 1
                ins.then_inc(dve_chain, 1)
                dve.wait_ge(dve_chain, chain[0])

            def layernorm(n, hN=hN):
                for t in range(NT):
                    for a in range(2):
                        last = nc.vector.bn_stats(ln_st[:, t, a, :], x_sb[:, t, a * HALF:(a + 1) * HALF])
                link(last)
                for t in range(NT):
                    last = nc.vector.bn_aggr(ln_mv[:, t, :], ln_st[:, t, :, :].rearrange("p a s -> p (a s)"))
                link(last)
                nc.vector.tensor_scalar(ln_var[:, :], ln_mv[:, :, 1], EPS, None, ALU.add).then_inc(ln_var_ready[n], 1)
                dve.wait_ge(ln_sd_ready[n], 1)
                link(nc.vector.reciprocal(ln_rs[:, :], ln_sd[:, :]))
                for t in range(NT):
                    nc.vector.tensor_scalar(hN[:, t, :], x_sb[:, t, :], ln_mv[:, t, 0:1], ln_rs[:, t:t + 1],
                                            ALU.subtract, ALU.mult).then_inc(ln_h_ready[n], 1)

            def layernorm_drain(n, scale, hT=hT):
                for t in range(NT):
                    dve.wait_ge(lnT_ps[n], 2 * t + 2)
                    nc.vector.tensor_scalar(hT[:, 4:8, t * P:(t + 1) * P],
                                            ps[:, 2 * t + 1, :].rearrange("p (c q) -> p c q", c=4),
                                            scale, None, ALU.mult).then_inc(lnT_dve[n], 1)

            nc.vector.memset(onesf[:, :], 1.0).then_inc(ones_set, 1)
            nc.vector.memset(onesb[:, :], 1.0).then_inc(ones_set, 1)
            link(nc.vector.memset(work[:, :], -1.0))
            dve.wait_ge(mask_in, 16)
            nc.vector.tensor_reduce(any_blk[:, :], mask_blocks[:, :], X, ALU.max).then_inc(any_ready, 1)
            dve.wait_ge(consts_in, 16)
            nc.vector.tensor_copy(identb[:, :], ident).then_inc(constb_set, 1)
            nc.vector.tensor_copy(upperb[:, :], cst[:, C_UP:C_UP + P]).then_inc(constb_set, 1)
            nc.vector.tensor_copy(causalb[:, :], cst[:, C_CAUS:C_CAUS + P]).then_inc(constb_set, 1)
            dve.wait_ge(any_ps, 1)
            nc.vector.tensor_scalar(valid[:, :], ps[:, 6, 64:65], 1.0, None, ALU.min)
            link(nc.vector.tensor_copy(work[:, 0:NBLK], ps[0:1, 6, 0:NBLK]))
            for r in range(NLIST // 8):
                src, dst = (work, work2) if r % 2 == 0 else (work2, work)
                link(nc.vector.max(order[:, 8 * r:8 * r + 8], src[:, :]))
                link(nc.vector.match_replace(dst[:, :], order[:, 8 * r:8 * r + 8], src[:, :], -1.0))
            nc.vector.tensor_scalar(pair_on[:, :], order[:, 0:NLIST:2], 0.0, None, ALU.is_gt)
            nc.vector.tensor_scalar(mask_ix[:, :], order[:, :], 0.0, None, ALU.max)
            link(nc.vector.tensor_scalar(ctx_ix[:, :], order[:, :], 1.0, 0.0, ALU.subtract, ALU.max))
            link(nc.vector.tensor_reduce(pairs_f[:, :], pair_on[:, :], X, ALU.add))
            nc.vector.tensor_scalar(pairs_i[:, :], pairs_f[:, :], 1.0, None, ALU.max).then_inc(list_ready, 1)

            nc.vector.memset(run_max[:, :], -3e38)
            nc.vector.memset(run_sum[:, :], 0.0)
            nc.vector.memset(o_acc, 0.0)
            dve.wait_ge(x_in, 16)
            layernorm(0)
            layernorm_drain(0, 1.0 / 32)
            for b in (t_drained[1], o_added[0], o_added[1]):
                dve.sem_inc(b, 1)

            pairs = dve.value_load(pairs_i[0:1, 0:1], min_val=1, max_val=NLIST // 2)
            with dve.Fori(0, pairs) as i:
                for b in range(2):
                    dve.wait_ge(mrow_in[b], 16 * i + 16)
                    nc.vector.tensor_scalar(bias_row[0:1, b, :].rearrange("o (j p) -> o j p", j=KJ),
                                            mask_row[0:1, b, :].rearrange("o (p j) -> o j p", j=KJ),
                                            -NEG, NEG, ALU.mult, ALU.add).then_inc(bias_ready, 1)
                for b in range(2):
                    for c in range(1, NC, 2):
                        dve.wait_ge(t_filled[1], 10 * i + 4 * b + c // 2 + 1)
                        nc.vector.tensor_copy(kT[b][:, c, :], ps[:, 5, :]).then_inc(t_drained[1], 1)
                for q in range(NT):
                    one = slice(q, q + 1)
                    dve.wait_ge(s_ready[q], i + 1)
                    nc.vector.tensor_reduce(blk_max[:, one], ps[:, 2 * q:2 * q + 2, :], mybir.AxisListType.XY, ALU.max)\
                        .then_inc(blk_max_ready[q], 1)
                    dve.wait_ge(blk_max_ready[q], i + 1)
                    nc.vector.tensor_tensor(new_max[:, one], run_max[:, one], blk_max[:, one], ALU.max)\
                        .then_inc(new_max_ready[q], 1)
                    dve.wait_ge(new_max_ready[q], i + 1)
                    nc.vector.tensor_scalar(neg_max[:, one], new_max[:, one], -1.0, None, ALU.mult)\
                        .then_inc(exp_args_ready[q], 1)
                    nc.vector.tensor_tensor(old_less_new[:, one], run_max[:, one], new_max[:, one], ALU.subtract)\
                        .then_inc(exp_args_ready[q], 1)
                for q in range(NT):
                    dve.wait_ge(t_filled[1], 10 * i + 8 + q + 1)
                    nc.vector.tensor_copy(probT[:, q, HALF:2 * HALF], ps[:, 5, :]).then_inc(t_drained[1], 1)
                for q in range(NT):
                    one = slice(q, q + 1)
                    dve.wait_ge(p_ready[q], i + 1)
                    nc.vector.scalar_tensor_tensor(out=run_sum[:, one], in0=run_sum[:, one], scalar=alpha[:, one],
                                                   in1=row_sum[:, one], op0=ALU.mult, op1=ALU.add)
                    nc.vector.tensor_copy(run_max[:, one], new_max[:, one])
                    dve.wait_ge(pv_ready[q], i + 1)
                    acc = o_acc[:, q, :].rearrange("p (a d) -> p a d", a=2)
                    bank = 6 if q == 0 else 0
                    nc.vector.scalar_tensor_tensor(out=acc, in0=acc, scalar=alpha[:, one], in1=ps[:, bank:bank + 2, :],
                                                   op0=ALU.mult, op1=ALU.add).then_inc(o_added[q], 1)
            for q in range(NT):
                dve.wait_ge(o_added[q], pairs + 1)
            link(nc.vector.reciprocal(inv_sum[:, :], run_sum[:, :]))
            link(nc.vector.tensor_scalar(inv_valid[:, :], inv_sum[:, :], valid[:, 0:1], None, ALU.mult))
            for t in range(NT):
                last = nc.vector.scalar_tensor_tensor(out=x_sb[:, t, :], in0=o_acc[:, t, :], scalar=inv_valid[:, t:t + 1],
                                                      in1=x_sb[:, t, :], op0=ALU.mult, op1=ALU.add)
            link(last)

            layernorm(1)
            layernorm_drain(1, 1.0)
            dve.wait_ge(proj_ps, 2)
            nc.vector.tensor_copy(compT, ps[:, 5, :].rearrange("p (k t) -> p k t", k=NR)).then_inc(compT_ready, 1)

            def rotate(out_even, out_odd, even, odd, cosv, sinv, shape):
                n = shape[0] * shape[1]
                tmp = [rope_tmp[:, k, 0:n].rearrange("p (a b) -> p a b", a=shape[0]) for k in range(4)]
                nc.vector.tensor_tensor(tmp[0], even, cosv, ALU.mult)
                nc.vector.tensor_tensor(tmp[1], odd, sinv, ALU.mult)
                nc.vector.tensor_tensor(tmp[2], even, sinv, ALU.mult)
                link(nc.vector.tensor_tensor(tmp[3], odd, cosv, ALU.mult))
                nc.vector.tensor_tensor(out_even, tmp[0], tmp[1], ALU.subtract)
                return nc.vector.tensor_tensor(out_odd, tmp[2], tmp[3], ALU.add)

            dve.wait_ge(kpe_ps, 1)
            kv = ps[:, 6, 0:NT * ROPE].rearrange("p (t i two) -> p t i two", t=NT, two=2)
            kr = k_rot.rearrange("p t u (i two) -> p t u i two", two=2)
            link(rotate(kr[:, :, 0, :, 0], kr[:, :, 0, :, 1], kv[:, :, :, 0], kv[:, :, :, 1], cos, sin, [NT, 32]))
            nc.vector.tensor_copy(k_rot[:, :, 1, :], k_rot[:, :, 0, :]).then_inc(k_rot_ready, 1)
            for t in range(NT):
                for a in range(2):
                    dve.wait_ge(qpe_ps, 2 * t + a + 1)
                    if t > 0:
                        dve.wait_ge(qpeT_ps, t)
                    if t + a > 0:
                        dve.wait_ge(q_rot_ready, 2 * t + a)
                    qv = ps[:, 2 * t + a, :].rearrange("p (h i two) -> p h i two", h=8, two=2)
                    qr = q_rot[:, 8 * a:8 * a + 8, :].rearrange("p h (i two) -> p h i two", two=2)
                    cosb = cos[:, t, :].unsqueeze(1).broadcast_to([P, 8, 32])
                    sinb = sin[:, t, :].unsqueeze(1).broadcast_to([P, 8, 32])
                    rotate(qr[:, :, :, 0], qr[:, :, :, 1], qv[:, :, :, 0], qv[:, :, :, 1], cosb, sinb, [8, 32])\
                        .then_inc(q_rot_ready, 1)
            for s in range(H + 4):
                if 0 <= s - 1 < H:
                    g = s - 1
                    dve.wait_ge(hs_ps, g + 1)
                    nc.vector.tensor_reduce(s_max[:, g % 2, 0:1], ps[:, 5, 0:P], X, ALU.max)
                    link(nc.vector.tensor_reduce(s_max[:, g % 2, 1:2], ps[:, 5, P:3 * P], X, ALU.max))
                    nc.vector.tensor_scalar(s_bias[:, g % 2, :], s_max[:, g % 2, :], -SCALE, None, ALU.mult)\
                        .then_inc(hmax_ready, 1)
                    dve.wait_ge(hexp_ready, g + 1)
                    link(nc.vector.reciprocal(s_inv[:, g % 2, :], s_sum[:, g % 2, :]))
                    nc.vector.tensor_scalar(p_sb[:, g % 2, 0, :], p_sb[:, g % 2, 0, :], s_inv[:, g % 2, 0:1], None, ALU.mult)
                    nc.vector.tensor_scalar(p_sb[:, g % 2, 1:3, :], p_sb[:, g % 2, 1:3, :], s_inv[:, g % 2, 1:2], None,
                                            ALU.mult).then_inc(hp_ready, 1)
                if 0 <= s - 2 < H:
                    g = s - 2
                    dve.wait_ge(pT_ps, g + 1)
                    nc.vector.tensor_copy(pT_sb[:, g % 2, :, :], ps[:, 6, 0:3 * P].rearrange("p (a k) -> p a k", a=3))\
                        .then_inc(pT_ready, 1)
            dve.wait_ge(wout_used, 4)
            for t in range(NT):
                for a in range(2):
                    xs = x_sb[:, t, a * HALF:(a + 1) * HALF]
                    last = nc.vector.tensor_tensor(xs, xs, ps[:, 2 * t + a, :], ALU.add)
                    last.then_inc(x2_ready, 1)
            dve.wait_ge(x2_ready, NT * 2)

            layernorm(2, fN)
            nc.vector.memset(ga[AR:AR + 1, :], 1.0)
            nc.vector.memset(gs[AR:AR + 1, :], 1.0)
            nc.vector.memset(ct_e, 0.0)
            nc.vector.memset(sel[:, :, E * SLOTS:(E + 1) * SLOTS].bitcast(F32), 0.0)
            layernorm_drain(2, 1.0, fT)
            for t in range(NT):
                dve.wait_ge(norm_hi, t + 1)
                nc.vector.tensor_tensor(hN_s[1][:, t, :], fN[:, t, :], hN_s[0][:, t, :].bitcast(F32), ALU.subtract)\
                    .then_inc(norm_lo, 1)
            dve.wait_ge(norm_lo, NT)
            nc.vector.memset(y_sb, 0.0)
            dve.wait_ge(gate_ps, 1)
            link(nc.vector.tensor_reduce(g_max[:, :], ps[:, 4, 0:NT * E].rearrange("p (t e) -> p t e", t=NT), X, ALU.max))
            nc.vector.tensor_scalar(g_neg[:, :], g_max[:, :], -1.0, None, ALU.mult).then_inc(g_neg_ready, 1)
            dve.wait_ge(g_exp_ready, NT)
            link(nc.vector.reciprocal(g_inv[:, :], g_sum[:, :]))
            for t in range(NT):
                last = nc.vector.tensor_scalar(probs[:, t, :], g_exp[:, t, :], g_inv[:, t:t + 1], None, ALU.mult)
            link(last)
            for t in range(NT):
                last = nc.vector.max(top_v[:, t, :], probs[:, t, :])
            link(last)
            for t in range(NT):
                last = nc.vector.max_index(top_i[:, t, :], top_v[:, t, :], probs[:, t, :])
            link(last)
            link(nc.vector.tensor_copy(top_f[:, :, :], top_i[:, :, :]))
            for t in range(NT):
                for k in range(TOPK):
                    last = nc.vector.tensor_scalar(onehot[:, t, :, k], cst[:, C_I8:C_I8 + E], top_f[:, t, k:k + 1], None,
                                                   ALU.is_equal)
            link(last)
            flat = onehot[:, :, :, :].rearrange("p t e k -> p t (e k)")
            nc.vector.tensor_copy(onehotb[:, :, :], flat).then_inc(onehot_ready, 1)
            link(nc.vector.tensor_scalar(far[:, :, :], flat, -1000.0, 1000.0, ALU.mult, ALU.add))
            dve.wait_ge(pos_ps, 1)
            link(nc.vector.tensor_tensor(slot[:, :, :], far[:, :, :],
                                         ps[:, 5, 0:NT * E * TOPK].rearrange("p (t n) -> p t n", t=NT), ALU.add))
            for t in range(NT):
                last = nc.vector.tensor_tensor(sel[:, t, 0:E * SLOTS].rearrange("p (n s) -> p n s", s=CAP),
                                               cst[:, C_I40:C_I40 + CAP].unsqueeze(1).broadcast_to([P, E * TOPK, CAP]),
                                               slot[:, t, :].unsqueeze(2).broadcast_to([P, E * TOPK, CAP]), ALU.is_equal)
            link(last)
            for t in range(NT):
                for k in range(TOPK):
                    one = [v.rearrange("p (e k s) -> p e k s", e=E, k=TOPK)[:, :, k, :]
                           for v in (sel[:, t, 0:E * SLOTS].bitcast(F32), selw[:, t, :])]
                    nc.vector.tensor_scalar(one[1], one[0], top_v[:, t, k:k + 1], None, ALU.mult).then_inc(sel_ready, 1)

            dve.wait_ge(norm_hi, 2 * NT)
            for t in range(NT):
                at = (slice(None), slice(None), slice(t * P, (t + 1) * P))
                nc.vector.tensor_tensor(hT_s[1][at], fT[at], hT_s[0][at].bitcast(F32), ALU.subtract).then_inc(norm_lo, 1)

            def gathered_lo(count):
                dve.wait_ge(xs_hi_done, 2 * count)
                nc.vector.tensor_tensor(xs_s[1][:, :, :].rearrange("p (a c) s -> p a (c s)", a=2), ps[:, 0:2, 0:4 * SLOTS],
                                        xs_s[0][:, :, :].bitcast(F32).rearrange("p (a c) s -> p a (c s)", a=2), ALU.subtract)\
                    .then_inc(xs_ready, 1)

            for s in (y_ready, ct_ready, sh_added):
                dve.sem_inc(s, 1)
            dve.wait_ge(b1T_ready, 1)
            gathered_lo(1)
            dve.wait_ge(combT_ready, 4)

            def add_expert(e):
                for r in range(2 * NT):
                    dve.wait_ge(comb_ps, 4 * e + r + 1)
                    to = x_sb[:, r // 2, (r % 2) * HALF:(r % 2 + 1) * HALF]
                    nc.vector.tensor_tensor(to, to, ps[:, (5, 6, 7, 5)[r], :], ALU.add).then_inc(comb_added, 1)

            with dve.Fori(0, E) as e:
                for n in range(NHALF):
                    at = NHALF * e + n
                    dve.wait_ge(w_hi_done, at + 1)
                    nc.vector.tensor_tensor(w_s[1][:, n % SPLIT, :], raw[:, n % RAW, :], w_s[0][:, n % SPLIT, :].bitcast(F32),
                                            ALU.subtract).then_inc(w_lo_done, 1)
                    if n == 0:
                        dve.wait_ge(sgelu_done, e + 1)
                        nc.vector.tensor_copy(b1_e[:, 0:NF], b1T[:, bass.ds(e * NF, NF)])
                        nc.vector.tensor_copy(b1_e[:, NF:NF + 4], b1T[:, bass.ds(e * 4 + E * NF, 4)]).then_inc(b1e_ready, 1)
                    for k in range(STEPS):
                        if n == FIRST_HALF["w1", k] + 4:
                            dve.wait_ge(gelu_done, STEPS * e + k + 1)
                            nc.vector.tensor_copy(hid_s[0][:, k % 2, :, :], hid).then_inc(hid_hi_done, 1)
                            dve.wait_ge(hid_hi_done, STEPS * e + k + 1)
                            nc.vector.tensor_tensor(hid_s[1][:, k % 2, :, :], hid, hid_s[0][:, k % 2, :, :].bitcast(F32),
                                                    ALU.subtract).then_inc(hid_ready, 1)
                    if n == 7:
                        add_expert(e)
                        dve.wait_ge(comb_ps, 4 * e + 4)
                        nc.vector.tensor_copy(ct_e, combT[:, bass.ds(e, 1), :].rearrange("p a t -> p (a t)")).then_inc(ct_ready, 1)
                    if n == FIRST_HALF["s1", 0] + 3:
                        dve.wait_ge(sgelu_done, e + 2)
                        nc.vector.tensor_copy(shid_s[0][:, :, :], shid).then_inc(shid_hi_done, 1)
                        dve.wait_ge(shid_hi_done, e + 1)
                        nc.vector.tensor_tensor(shid_s[1][:, :, :], shid, shid_s[0][:, :, :].bitcast(F32), ALU.subtract)\
                            .then_inc(shid_ready, 1)
                    if n == NHALF - 2:
                        gathered_lo(e + 2)
                dve.wait_ge(y_ps, e + 1)
                nc.vector.tensor_copy(y_sb, ps[0:SLOTS, 3:5, :]).then_inc(y_ready, 1)
                dve.wait_ge(w_used, NHALF * (e + 1) + SPLIT)
                for r in range(2 * NT):
                    to = x_sb[:, r // 2, (r % 2) * HALF:(r % 2 + 1) * HALF]
                    nc.vector.scalar_tensor_tensor(out=to, in0=ps[:, (5, 6, 7, 2)[r], :], scalar=0.2, in1=to,
                                                   op0=ALU.mult, op1=ALU.add).then_inc(sh_added, 1)
            add_expert(E)
            dve.wait_ge(comb_added, 4 * E + 4)
            for r in range(2 * NT):
                t, a = r // 2, r % 2
                dve.wait_ge(sh_ps, r + 1)
                nc.vector.scalar_tensor_tensor(out=out_sb[:, t, a * HALF:(a + 1) * HALF], in0=ps[:, (5, 6, 7, 2)[r], :], scalar=0.2,
                                               in1=x_sb[:, t, a * HALF:(a + 1) * HALF], op0=ALU.mult, op1=ALU.add)\
                    .then_inc(out_ready, 1)

        @block.tensor
        def _(pe):
            mm, turn = nc.tensor.matmul, nc.tensor.transpose

            def layernorm_turn(n, hN=hN):
                for t in range(NT):
                    pe.wait_ge(ln_h_ready[n], t + 1)
                    for a in range(2):
                        for c in range(4):
                            cc = 4 * a + c
                            last = turn(ps[:, 2 * t + a, c * P:(c + 1) * P], hN[:, t, cc * P:(cc + 1) * P], ident)
                        last.then_inc(lnT_ps[n], 1)
                pe.wait_ge(lnT_act[n], NT)
                pe.wait_ge(lnT_dve[n], NT)

            pe.sem_inc(pair_done, 1)
            pe.wait_ge(consts_in, 16)
            pe.wait_ge(ones_set, 2)
            pe.wait_ge(any_ready, 1)
            mm(ps[0:1, 6, 0:NBLK], any_blk[:, :], cst[0:NBLK, C_BNO:C_BNO + NBLK], start=True, stop=True)
            mm(ps[:, 6, 64:65], onesf[0:NBLK, :], any_blk[:, :], start=True, stop=True).then_inc(any_ps, 1)
            layernorm_turn(0)
            pe.wait_ge(small_in, 32)
            for a in range(2):
                turn(ps[:, 7, a * P:(a + 1) * P], b1_raw[:, a, :], ident)
            turn(ps[:, 7, 2 * P:2 * P + NF], b1_raw[0:NF, 2, :], ident[0:NF, 0:NF]).then_inc(b1_ps, 1)
            pe.wait_ge(b1T_ready, 1)

            pe.wait_ge(list_ready, 1)
            pairs = pe.value_load(pairs_i[0:1, 0:1], min_val=1, max_val=NLIST // 2)
            with pe.Fori(0, pairs) as i:
                def turn_keys(b, c):
                    if c == 0:
                        pe.wait_ge(ctx_in[b], 16 * i + 16)
                    pe.wait_ge(t_drained[c % 2], 10 * i + 4 * b + c // 2 + 1)
                    for j in range(KJ):
                        last = turn(ps[:, 4 + c % 2, j * P:(j + 1) * P], ctx_t[b][:, j, c * P:(c + 1) * P], ident)
                    last.then_inc(t_filled[c % 2], 1)

                def score(b, c):
                    pe.wait_ge(t_drained[c % 2], 10 * i + 4 * b + c // 2 + 2)
                    for q in range(NT):
                        mm(ps[:, 2 * q + b, :], hT[:, c, q * P:(q + 1) * P], kT[b][:, c, :], start=(c == 0), stop=False)

                pe.wait_ge(o_added[1], i + 1)
                for b in range(2):
                    turn_keys(b, 0)
                    turn_keys(b, 1)
                    for c in range(NC):
                        score(b, c)
                        if c + 2 < NC:
                            turn_keys(b, c + 2)
                pe.wait_ge(bias_ready, 2 * i + 2)
                for q in range(NT):
                    for b in range(2):
                        last = mm(ps[:, 2 * q + b, :], onesb[0:1, :], bias_row[0:1, b, :], start=False, stop=True)
                    last.then_inc(s_ready[q], 1)
                for q in range(NT):
                    pe.wait_ge(p_ready[q], i + 1)
                    for b in range(2):
                        pe.wait_ge(t_drained[b], 10 * i + 8 + q + 1)
                        for j in range(KJ):
                            last = turn(ps[:, 4 + b, j * P:(j + 1) * P], prob[:, q, (KJ * b + j) * P:(KJ * b + j + 1) * P], ident)
                        last.then_inc(t_filled[b], 1)
                    if q == 0:
                        pe.wait_ge(o_added[0], i + 1)
                    bank = 6 if q == 0 else 0
                    for b in range(2):
                        pe.wait_ge(t_drained[b], 10 * i + 8 + q + 2)
                        for j in range(KJ):
                            for a in range(2):
                                last = mm(ps[:, bank + a, :], probT[:, q, (KJ * b + j) * P:(KJ * b + j + 1) * P],
                                          ctx_t[b][:, j, a * HALF:(a + 1) * HALF],
                                          start=(b == 0 and j == 0), stop=(b == 1 and j == KJ - 1))
                    last.then_inc(pv_ready[q], 1)
                pe.wait_ge(pv_ready[1], i + 1)
                pe.sem_inc(pair_done, 1)

            layernorm_turn(1)
            pe.wait_ge(wq_in, 32)
            for m in range(NR):
                for c in range(NC):
                    last = mm(ps[:, 4, m * TOK:(m + 1) * TOK], wqa_sb[:, c, m * P:(m + 1) * P], hT[:, c, :],
                              start=(c == 0), stop=(c == NC - 1))
            last.then_inc(proj_ps, 1)
            pe.wait_ge(wkv_in, 32)
            for m in range(NR):
                for c in range(NC):
                    last = mm(ps[:, 5, m * TOK:(m + 1) * TOK], wkva_sb[:, c, m * P:(m + 1) * P], hT[:, c, :],
                              start=(c == 0), stop=(c == NC - 1))
            last.then_inc(proj_ps, 1)
            for t in range(NT):
                for c in range(NC):
                    last = mm(ps[:, 6, t * ROPE:(t + 1) * ROPE], hT[:, c, t * P:(t + 1) * P], wkva_sb[:, c, RANK:RANK + ROPE],
                              start=(c == 0), stop=(c == NC - 1))
            last.then_inc(kpe_ps, 1)
            pe.wait_ge(qaT_ready, 1)
            for t in range(NT):
                for a in range(2):
                    for k in range(NR):
                        last = mm(ps[:, 2 * t + a, :].rearrange("p (h n) -> p h n", h=8), qaT[:, k, t * P:(t + 1) * P],
                                  wqb_sb[:, k, 8 * a:8 * a + 8, NOPE:QH], start=(k == 0), stop=(k == NR - 1))
                    last.then_inc(qpe_ps, 1)
            pe.wait_ge(compT_ready, 1)
            for n in range(2 * NT * 2):
                if n >= 2:
                    pe.wait_ge(v_ready, n - 1)
                for k in range(NR):
                    last = mm(ps[:, 4 + n % 2, :].rearrange("p (h v) -> p h v", h=4), compT[:, k, (n // 4) * P:(n // 4 + 1) * P],
                              wkvb_sb[:, k, 4 * (n % 4):4 * (n % 4) + 4, NOPE:2 * NOPE], start=(k == 0), stop=(k == NR - 1))
                last.then_inc(v_ps, 1)
            pe.wait_ge(k_rot_ready, 1)
            for t in range(NT):
                last = turn(ps[:, 7, t * P:(t + 1) * P], k_rot[:, t, :, :].rearrange("p u n -> p (u n)"), ident)
            last.then_inc(kpeT_ps, 1)
            for t in range(NT):
                pe.wait_ge(q_rot_ready, 2 * t + 2)
                for m in range(H // 2):
                    last = turn(ps[:, 2 * t + m // 4, (m % 4) * P:(m % 4 + 1) * P],
                                q_rot[:, 2 * m:2 * m + 2, :].rearrange("p h n -> p (h n)"), ident)
                last.then_inc(qpeT_ps, 1)
            pe.wait_ge(kpeT_ready, 1)
            pe.wait_ge(qpeT_ready, NT)
            pe.wait_ge(v_ready, 2 * NT * 2)
            pe.wait_ge(constb_set, 3)

            def head_project(g):
                if g >= 1:
                    pe.wait_ge(qk_ready, g)
                for k in range(NR):
                    mm(ps[:, 4, 0:TOK], wqb_sb[:, k, g, 0:NOPE], qaT[:, k, :], start=(k == 0), stop=(k == NR - 1))
                for k in range(NR):
                    last = mm(ps[:, 4, TOK:2 * TOK], wkvb_sb[:, k, g, 0:NOPE], compT[:, k, :],
                              start=(k == 0), stop=(k == NR - 1))
                last.then_inc(qk_ps, 1)

            def head_scores(g):
                pe.wait_ge(qk_ready, g + 1)
                if g >= 1:
                    pe.wait_ge(hexp_ready, g)
                r = slice(ROPE * (g % 2), ROPE * (g % 2) + ROPE)
                for t in range(NT):
                    to, keys = ps[:, 5, t * P:(2 * t + 1) * P], (t + 1) * P
                    mm(to, qkT[:, g % 2, t * P:(t + 1) * P], qkT[:, g % 2, TOK:TOK + keys], start=True, stop=False)
                    mm(to, q_peT[r, g // 2, t * P:(t + 1) * P], k_peT[r, 0:keys], start=False, stop=False)
                    last = mm(ps[:, 5, 2 * t * P:(2 * t + 1) * P], identb[:, :], causalb[:, :], start=False, stop=True)
                last.then_inc(hs_ps, 1)

            def head_turn(g):
                pe.wait_ge(hp_ready, g + 1)
                if g >= 1:
                    pe.wait_ge(pT_ready, g)
                for m in range(3):
                    last = turn(ps[:, 6, m * P:(m + 1) * P], p_sb[:, g % 2, m, :], ident)
                last.then_inc(pT_ps, 1)

            def head_values(g):
                pe.wait_ge(pT_ready, g + 1)
                if g >= 1:
                    pe.wait_ge(ho_ready, g)
                mm(ps[:, 7, 0:TOK], v_sb[:, 0, g, :], pT_sb[:, g % 2, 0:2, :].rearrange("p a k -> p (a k)"), start=True, stop=False)
                mm(ps[:, 7, P:TOK], v_sb[:, 1, g, :], pT_sb[:, g % 2, 2, :], start=False, stop=True).then_inc(ho_ps, 1)

            def head_out(g):
                pe.wait_ge(ho_ready, g + 1)
                if g % 4 == 0:
                    pe.wait_ge(wout_in[g // 4], 16)
                for t in range(NT):
                    for a in range(2):
                        last = mm(ps[:, 2 * t + a, :], attnT[:, g, t * P:(t + 1) * P], wout_sb[:, g, a * HALF:(a + 1) * HALF],
                                  start=(g == 0), stop=(g == H - 1))
                if g % 4 == 3:
                    last.then_inc(wout_used, 1)

            for s in range(H + 4):
                for lag, stage in enumerate((head_project, head_scores, head_turn, head_values, head_out)):
                    if 0 <= s - lag < H:
                        stage(s - lag)

            layernorm_turn(2, fN)
            pe.wait_ge(gate_in, 16)
            for t in range(NT):
                for c in range(NC):
                    last = mm(ps[:, 4, t * E:(t + 1) * E], fT[:, c, t * P:(t + 1) * P], gate_sb[:, c, :],
                              start=(c == 0), stop=(c == NC - 1))
            last.then_inc(gate_ps, 1)
            pe.wait_ge(wd_in, 16)
            for c in range(NC):
                last = mm(ps[0:AR, 7, 0:TOK], wd_sb[:, c, :], fT[:, c, :], start=(c == 0), stop=(c == NC - 1))
            last.then_inc(adapt_ps, 1)
            pe.wait_ge(onehot_ready, 1)
            n = E * TOPK
            mm(ps[:, 5, 0:n], upperb[:, :], onehotb[:, 0, :], start=True, stop=True)
            mm(ps[:, 5, n:2 * n], onesb[:, :], onehotb[:, 0, :], start=True, stop=False)
            mm(ps[:, 5, n:2 * n], upperb[:, :], onehotb[:, 1, :], start=False, stop=True).then_inc(pos_ps, 1)
            pe.wait_ge(sel_ready, NT * TOPK)
            for e in range(E):
                for t in range(NT):
                    at = (e % 2) * TOK + t * P
                    last = turn(ps[0:SLOTS, (4, 5, 6, 3)[e // 2], at:at + P], selw[:, t, e * SLOTS:(e + 1) * SLOTS], ident)
                if e % 2:
                    last.then_inc(combT_ps, 1)
            pe.wait_ge(norm_lo, 2 * NT)

            def gather(e):
                for c in range(NC):
                    for t in range(NT):
                        for part in range(2):
                            last = mm(ps[:, c // 4, (c % 4) * SLOTS:(c % 4 + 1) * SLOTS], hN_s[part][:, t, c * P:(c + 1) * P],
                                      sel[:, t, bass.ds(e * SLOTS, SLOTS)], start=(t == 0 and part == 0), stop=(t == 1 and part == 1))
                last.then_inc(gather_ps, 1)

            def combine(e):
                pe.wait_ge(y_ready, e + 1)
                pe.wait_ge(ct_ready, e + 1)
                for r in range(2 * NT):
                    if r == 3:
                        pe.wait_ge(comb_added, 4 * e + 1)
                    mm(ps[:, (5, 6, 7, 5)[r], :], ct_e[:, (r // 2) * P:(r // 2 + 1) * P], y_sb[:, r % 2, :],
                       start=True, stop=True).then_inc(comb_ps, 1)

            pe.sem_inc(w_used, SPLIT)
            gather(0)
            pe.wait_ge(combT_ready, 4)
            pe.wait_ge(gs_ready, 1)
            with pe.Fori(0, E) as e:
                pe.wait_ge(xs_ready, e + 1)
                pe.wait_ge(sh_added, 4 * e + 1)
                pe.wait_ge(wd_in, 16 * e + 32)
                for c in range(NC):
                    last = mm(ps[0:AR, 7, 0:SLOTS], wd_sb[:, c, :], xs[:, c, :], start=(c == 0), stop=(c == NC - 1))
                last.then_inc(adapt_ps, 1)
                for n in range(NHALF):
                    (kind, k), x = ROUND[n // 2], n % 2
                    hi, lo = (half_view(w[:, n % SPLIT, :], n) for w in w_s)
                    if kind == "w2" and x == 0:
                        pe.wait_ge(hid_ready, STEPS * e + k + 1)
                    if kind == "s2" and x == 0:
                        pe.wait_ge(shid_ready, e + 1)
                    pe.wait_ge(w_hi_done, NHALF * e + n + 1)
                    if kind == "w1":
                        to = ps[0:SLOTS, k % 2, :]
                        for c in range(4):
                            for part in range(2):
                                mm(to, xs_s[part][:, 4 * x + c, :], hi[:, c, :], start=(x == 0 and c == 0 and part == 0), stop=False)
                        pe.wait_ge(w_lo_done, NHALF * e + n + 1)
                        for c in range(4):
                            last = mm(to, xs_s[0][:, 4 * x + c, :], lo[:, c, :], start=False, stop=(x == 1 and c == 3))
                    elif kind == "w2":
                        for j in range(2):
                            for part in range(2):
                                for a in range(2):
                                    mm(ps[0:SLOTS, 3 + a, :], hid_s[part][:, k % 2, 2 * x + j, :], hi[:, j, a * HALF:(a + 1) * HALF],
                                       start=(k == 0 and x == 0 and j == 0 and part == 0), stop=False)
                        pe.wait_ge(w_lo_done, NHALF * e + n + 1)
                        for j in range(2):
                            for a in range(2):
                                last = mm(ps[0:SLOTS, 3 + a, :], hid_s[0][:, k % 2, 2 * x + j, :], lo[:, j, a * HALF:(a + 1) * HALF],
                                          start=False, stop=False)
                    elif kind == "s1":
                        pe.wait_ge(w_lo_done, NHALF * e + n + 1)
                        for j in range(2):
                            for c in range(NC):
                                for w, act_part in ((hi, 0), (hi, 1), (lo, 0)):
                                    last = mm(ps[:, 5 + x, j * TOK:(j + 1) * TOK], w[:, c, j * P:(j + 1) * P],
                                              hT_s[act_part][:, c, :], start=(c == 0 and act_part == 0 and w is hi),
                                              stop=(c == NC - 1 and w is lo))
                    else:
                        for w, parts in ((hi, (0, 1)), (lo, (0,))):
                            if w is lo:
                                pe.wait_ge(w_lo_done, NHALF * e + n + 1)
                            for j in range(2):
                                for part in parts:
                                    for r in range(2 * NT):
                                        last = mm(ps[:, (5, 6, 7, 2)[r], :], shid_s[part][:, 2 * x + j, (r // 2) * P:(r // 2 + 1) * P],
                                                  w[:, j, (r % 2) * HALF:(r % 2 + 1) * HALF],
                                                  start=(x == 0 and j == 0 and part == 0 and w is hi), stop=(x == 1 and j == 1 and w is lo))
                    last.then_inc(w_used, 1)
                    for q in range(STEPS):
                        if n == FIRST_HALF["w1", q] + 2:
                            pe.wait_ge(a_copied, STEPS * e + q + 1)
                            for j in range(4):
                                last = turn(ps[:, 2, j * SLOTS:(j + 1) * SLOTS], a_sb[:, j * P:(j + 1) * P], ident[0:SLOTS, 0:SLOTS])
                            last.then_inc(a_turned, 1)
                    if n == 5:
                        pe.wait_ge(ga_ready, e + 1)
                        combine(e)
                    if n == FIRST_HALF["s1", 0] + 1:
                        gather(e + 1)
                    if n == FIRST_HALF["w2", STEPS - 1] + 1:
                        pe.wait_ge(wub_in, 32 * e + 32)
                        for a in range(2):
                            last = mm(ps[0:SLOTS, 3 + a, :], ga, wub_sb[:, a, :], start=False, stop=True)
                        last.then_inc(y_ps, 1)
            pe.wait_ge(sh_added, 4 * E + 1)
            combine(E)
            pe.wait_ge(wub_in, 32 * E + 32)
            pe.wait_ge(comb_added, 4 * E + 4)
            for r in range(2 * NT):
                mm(ps[:, (5, 6, 7, 2)[r], :], gs[:, (r // 2) * P:(r // 2 + 1) * P], wub_sb[:, r % 2, :], start=True, stop=True)\
                    .then_inc(sh_ps, 1)


_INS = ['x', 'ctx_2048', 'mask', 'L0_attn_Wqa', 'L0_attn_Wqb', 'L0_attn_Wkva', 'L0_attn_Wkvb', 'L0_attn_Wout',
        'L0_ffn_gate_w', 'L0_ffn_w1', 'L0_ffn_b1', 'L0_ffn_w2', 'L0_ffn_b2', 'L0_ffn_wd', 'L0_ffn_wu', 'L0_ffn_sw1',
        'L0_ffn_sb1', 'L0_ffn_sw2', 'L0_ffn_sb2', 'L0_ffn_swd', 'L0_ffn_swu', 'consts']
_OUTS = [((1, TOK, D), 'float32')]


def constants(np):
    c = np.zeros((P, NCONST), np.float32)
    c[:, C_ID:C_ID + P] = np.eye(P)
    c[:, C_UP:C_UP + P] = np.triu(np.ones((P, P)), 1)
    c[:, C_CAUS:C_CAUS + P] = np.triu(np.full((P, P), NEG), 1)
    theta = np.float32(10000.0) ** (np.float32(-2.0) * np.arange(ROPE // 2, dtype=np.float32) / np.float32(ROPE))
    angle = (np.arange(TOK, dtype=np.float32)[:, None] * theta[None, :].astype(np.float32)).astype(np.float32)
    for t in range(NT):
        c[:, C_COS + 32 * t:C_COS + 32 * t + 32] = np.cos(angle[t * P:(t + 1) * P])
        c[:, C_SIN + 32 * t:C_SIN + 32 * t + 32] = np.sin(angle[t * P:(t + 1) * P])
    c[:, C_I8:C_I8 + E] = np.arange(E)
    c[:, C_I40:C_I40 + CAP] = np.arange(CAP)
    c[0:NBLK, C_BNO:C_BNO + NBLK] = np.diag(np.arange(1, NBLK + 1))
    return c


def kernel(**inputs):
    import numpy as _np
    import concourse.bacc as _bacc
    from concourse import mybir as _mybir
    from concourse.bass_utils import run_bass_kernel_spmd as _run

    given = dict(inputs)
    given['mask'] = _np.concatenate([_np.zeros(HALF, bool), _np.asarray(inputs['mask_BxS2_bk0']).reshape(-1)])
    given['ctx_2048'] = _np.asarray(inputs['ctx_2048']).reshape(KEYS, D)
    given['consts'] = constants(_np)
    nc = _bacc.Bacc("TRN2", target_bir_lowering=False, num_devices=1)
    arrays, args = {}, []
    for name in _INS:
        a = _np.ascontiguousarray(given[name])
        arrays[f"in_{name}_dram"] = a
        args.append(nc.dram_tensor(f"in_{name}_dram", a.shape, _mybir.dt.from_np(a.dtype), kind="ExternalInput").ap())
    for i, (shape, dtype) in enumerate(_OUTS):
        dt = _mybir.dt.from_np(_np.dtype(dtype))
        args.append(nc.dram_tensor(f"out_{i}_dram", shape, dt, kind="ExternalOutput").ap())
    build(nc, *args)
    r = _run(nc, [arrays], core_ids=[0])
    got = tuple(r.results[0][f"out_{i}_dram"] for i in range(len(_OUTS)))
    return got[0]
```

```python
from contextlib import ExitStack

import concourse.bass as bass
from concourse import mybir

F32 = mybir.dt.float32
F32R = mybir.dt.float32r
BF16 = mybir.dt.bfloat16
I32 = mybir.dt.int32
U32 = mybir.dt.uint32
U8 = mybir.dt.uint8
ALU = mybir.AluOpType
ACT = mybir.ActivationFunctionType
X = mybir.AxisListType.X

P = 128
D = 1024
TOK = 256
NT = TOK // P
NC = D // P
HALF = 512
KEYS = 25088
NBLK = KEYS // HALF
KJ = HALF // P
NLIST = 56
H = 16
NOPE = 128
ROPE = 64
QH = NOPE + ROPE
RANK = 256
NR = RANK // P
E = 8
TOPK = 2
CAP = int(TOK * 1.25 / E)
SLOTS = TOPK * CAP
F = 4096
NF = F // P
AR = 32
TILE = 4096
HT = TILE // 2
STEPS = F // HALF
RAW = 6
SPLIT = 3
ROUND = [("s1", 0), ("w1", 0)] + [x for k in range(1, STEPS) for x in (("w1", k), ("w2", k - 1))]\
    + [("s2", 0), ("w2", STEPS - 1)]
NHALF = 2 * len(ROUND)
assert NHALF % RAW == 0 and NHALF % SPLIT == 0
FIRST_HALF = {tile: 2 * n for n, tile in enumerate(ROUND)}
COMBINE = 9
COMB_BANKS = (4, 3, 7, 2)
TURN = 3
S_BANKS = (5, 6, 7, 0)
NEG = -1e30
SCALE = QH ** -0.5
EPS = 1e-5

C_ID, C_UP, C_CAUS = 0, 128, 256
C_COS, C_SIN = 384, 448
C_I8, C_I40, C_BNO = 512, 520, 560
NCONST = 560 + NBLK


def build(nc, x, ctx, mask, Wqa, Wqb, Wkva, Wkvb, Wout, gate_w, w1, b1, w2, b2, wd, wu,
          sw1, sb1, sw2, sb2, swd, swu, consts, out):
    with ExitStack() as stack:
        def sb(name, shape, dt=F32):
            return stack.enter_context(nc.sbuf_tensor(name, shape, dt))

        def sem(name):
            return stack.enter_context(nc.semaphore(name))

        x_sb = sb("x_sb", [P, NT, D])
        cst = sb("cst", [P, NCONST])
        ident = cst[:, C_ID:C_ID + P]
        cos = cst[:, C_COS:C_COS + NT * 32].rearrange("p (t i) -> p t i", t=NT)
        sin = cst[:, C_SIN:C_SIN + NT * 32].rearrange("p (t i) -> p t i", t=NT)
        identb = sb("identb", [P, P], BF16)
        upperb = sb("upperb", [P, P], BF16)
        causalb = sb("causalb", [P, P], BF16)
        onesb = sb("onesb", [P, P], BF16)
        onesf = sb("onesf", [P, P])
        gate_sb = sb("gate_sb", [P, NC, E])
        b1T = sb("b1T", [P, (E + 1) * NF])
        ln_st = sb("ln_st", [P, NT, 2, 6])
        ln_mv = sb("ln_mv", [P, NT, 2])
        ln_var = sb("ln_var", [P, NT])
        ln_sd = sb("ln_sd", [P, NT])
        ln_rs = sb("ln_rs", [P, NT])
        mask_blocks = sb("mask_blocks", [NBLK, HALF], U8)
        any_blk = sb("any_blk", [NBLK, 1])
        work = sb("work", [1, NLIST])
        work2 = sb("work2", [1, NLIST])
        order = sb("order", [1, NLIST])
        pair_on = sb("pair_on", [1, NLIST // 2])
        pairs_f = sb("pairs_f", [1, 1])
        order_c = sb("order_c", [1, NLIST])
        mask_ix = sb("mask_ix", [1, NLIST], I32)
        ctx_ix = sb("ctx_ix", [1, NLIST], I32)
        pairs_i = sb("pairs_i", [1, 1], I32)
        slot_w = sb("slot_w", [SLOTS, E])
        slot_w_e = sb("slot_w_e", [SLOTS, 1])
        valid = sb("valid", [P, 1])
        run_max = sb("run_max", [P, NT])
        blk_max = sb("blk_max", [P, NT])
        new_max = sb("new_max", [P, NT])
        neg_max = sb("neg_max", [P, NT])
        old_less_new = sb("old_less_new", [P, NT])
        alpha = sb("alpha", [P, NT])
        row_sum = sb("row_sum", [P, NT])
        run_sum = sb("run_sum", [P, NT])
        inv_sum = sb("inv_sum", [P, NT])
        inv_valid = sb("inv_valid", [P, NT])
        s_max = sb("s_max", [P, 2, NT])
        s_bias = sb("s_bias", [P, 2, NT])
        s_sum = sb("s_sum", [P, 2, NT])
        s_inv = sb("s_inv", [P, 2, NT])
        b1_e = sb("b1_e", [P, NF + 4])
        g_max = sb("g_max", [P, NT])
        g_neg = sb("g_neg", [P, NT])
        g_exp = sb("g_exp", [P, NT, E])
        g_sum = sb("g_sum", [P, NT])
        g_inv = sb("g_inv", [P, NT])
        probs = sb("probs", [P, NT, E])
        top_v = sb("top_v", [P, NT, 8])
        top_i = sb("top_i", [P, NT, 8], U32)
        top_f = sb("top_f", [P, NT, 8])
        onehot = sb("onehot", [P, NT, E, TOPK])
        onehotb = sb("onehotb", [P, NT, E * TOPK], BF16)
        far = sb("far", [P, NT, E * TOPK])
        slot = sb("slot", [P, NT, E * TOPK])
        early = ExitStack()

        def sb_early(name, shape, dt=F32):
            return early.enter_context(nc.sbuf_tensor(name, shape, dt))

        ring = sb_early("ring", [P, 8, TILE])
        arena = sb_early("arena", [P, 10752])
        projecting = ExitStack()
        h = projecting.enter_context(nc.sbuf_tensor("h", [P, 2 * NT * D], F32))
        hN = h[:, 0:NT * D].rearrange("p (t d) -> p t d", t=NT)
        hT = h[:, NT * D:2 * NT * D].rearrange("p (c t) -> p c t", c=NC)

        def part_of(memory):
            def part(at, shape, rows=P):
                n = 1
                for s in shape:
                    n *= s
                v = memory[0:rows, at:at + n]
                if len(shape) == 2:
                    return v.rearrange("p (a b) -> p a b", a=shape[0])
                if len(shape) == 3:
                    return v.rearrange("p (a b c) -> p a b c", a=shape[0], b=shape[1])
                return v
            return part

        part = part_of(arena)

        o_acc = part(0, [NT, D])
        prob = part(2048, [NT, 2 * HALF])
        probT = part(4096, [NT, 2 * KJ * P])
        b1_raw = part(9728, [3, P])
        mask_row = arena[0:1, 6144:6400].bitcast(U8).rearrange("p (b n) -> p b n", b=2)
        bias_row = arena[0:1, 6400:6912].bitcast(BF16).rearrange("p (b n) -> p b n", b=2)
        kT = [ring[:, 2 + b, :].rearrange("p (c k) -> p c k", c=NC) for b in range(2)]
        ctx_t = [ring[:, b, :].rearrange("p (j d) -> p j d", j=KJ) for b in range(2)]

        tail4 = ring[:, 4:8, :].rearrange("p s n -> p (s n)")
        wqb_sb = tail4[:, 0:6144].rearrange("p (k h n) -> p k h n", k=NR, h=H)
        wkvb_sb = tail4[:, 6144:14336].rearrange("p (k h n) -> p k h n", k=NR, h=H)
        wqa_sb = tail4[:, 14336:16384].rearrange("p (c n) -> p c n", c=NC)
        wkva_sb = part(7168, [NC, RANK + ROPE])
        wout_sb = ring[:, 0:4, :].rearrange("p s (h n) -> p (s h) n", h=4)
        qaT = part(0, [NR, TOK])
        compT = part(512, [NR, TOK])
        q_rot = part(1024, [H, ROPE])
        rope_tmp = part(2048, [4, 256])
        q_peT = part(3072, [H // 2, TOK])
        k_rot = part(5120, [NT, 2, ROPE])
        k_peT = part(5376, [TOK])
        qkT = part(5632, [2, 2 * TOK])
        v_sb = part(6656, [NT, H, NOPE])
        p_sb = part(1024, [2, 3, P])
        pT_sb = part(2048, [2, 3, P])

        projecting.close()
        attn_s = [sb_early(f"attn_{n}", [P, 2, TOK], F32R) for n in ("hi", "lo")]
        wout_s = [sb_early(f"wout_{n}", [P, 2, D], F32R) for n in ("hi", "lo")]

        early.close()
        hT_s = [sb(f"hT_{n}", [P, NC, TOK], F32R) for n in ("hi", "lo")]
        w_s = [sb(f"w_{n}", [P, SPLIT, HT], F32R) for n in ("hi", "lo")]
        raw = sb("raw", [P, RAW, HT])
        sel = sb("sel", [P, NT, E * SLOTS])
        xs_s = [sb(f"xs_{n}", [P, NC, SLOTS], F32R) for n in ("hi", "lo")]
        hid_s = [sb(f"hid_{n}", [P, 2, 4, SLOTS], F32R) for n in ("hi", "lo")]
        shid_s = [sb(f"shid_{n}", [P, 4, TOK], F32R) for n in ("hi", "lo")]
        y_s = [sb(f"y_{n}", [SLOTS, 2, HALF], F32R) for n in ("hi", "lo")]
        ct_e = sb("ct_e", [SLOTS, TOK], F32R)
        late = sb("late", [P, 9488])
        late_part = part_of(late)
        fN = late_part(0, [NT, D])
        a_sb = late_part(6992, [HALF], rows=SLOTS)
        fT = late_part(2048, [NC, TOK])
        combT = late_part(2048, [E, TOK], rows=SLOTS)
        selw = late_part(4096, [NT, E * SLOTS])
        shid = late_part(4096, [4, TOK])
        xs = late_part(7824, [NC, SLOTS])
        hid = late_part(7504, [4, SLOTS])
        wd_sb = late_part(5376, [NC, AR])
        wub_sb = late_part(5632, [2, HALF], rows=AR + 1)
        ga = late_part(6656, [SLOTS], rows=AR + 1)
        gs = late_part(6736, [TOK], rows=AR + 1)
        swub_sb = late_part(8464, [2, HALF], rows=AR + 1)
        ps = stack.enter_context(nc.psum_tensor("ps", [P, 8, HALF], F32))

        consts_in, x_in, mask_in, small_in = sem("consts_in"), sem("x_in"), sem("mask_in"), sem("small_in")
        dve_chain = sem("dve_chain")
        ones_set, constb_set = sem("ones_set"), sem("constb_set")
        any_ready, any_ps, list_ready = sem("any_ready"), sem("any_ps"), sem("list_ready")
        b1_ps, b1T_ready = sem("b1_ps"), sem("b1T_ready")
        ln_var_ready = [sem(f"ln_var_ready{n}") for n in range(3)]
        ln_sd_ready = [sem(f"ln_sd_ready{n}") for n in range(3)]
        ln_h_ready = [sem(f"ln_h_ready{n}") for n in range(3)]
        lnT_ps = [sem(f"lnT_ps{n}") for n in range(3)]
        lnT_act = [sem(f"lnT_act{n}") for n in range(3)]
        lnT_dve = [sem(f"lnT_dve{n}") for n in range(3)]
        ctx_in = [sem(f"ctx_in{b}") for b in range(2)]
        mrow_in = [sem(f"mrow_in{b}") for b in range(2)]
        bias_ready = sem("bias_ready")
        pair_done = sem("pair_done")
        t_filled = [sem(f"t_filled{b}") for b in range(2)]
        t_drained = [sem(f"t_drained{b}") for b in range(2)]
        s_ready = [sem(f"s_ready{q}") for q in range(NT)]
        blk_max_ready = [sem(f"blk_max_ready{q}") for q in range(NT)]
        new_max_ready = [sem(f"new_max_ready{q}") for q in range(NT)]
        exp_args_ready = [sem(f"exp_args_ready{q}") for q in range(NT)]
        p_ready = [sem(f"p_ready{q}") for q in range(NT)]
        pv_ready = [sem(f"pv_ready{q}") for q in range(NT)]
        o_added = [sem(f"o_added{q}") for q in range(NT)]
        wq_in, wkv_in, wout_in = sem("wq_in"), sem("wkv_in"), [sem(f"wout_in{s}") for s in range(4)]
        proj_ps, qaT_ready, compT_ready = sem("proj_ps"), sem("qaT_ready"), sem("compT_ready")
        kpe_ps, k_rot_ready, kpeT_ps, kpeT_ready = sem("kpe_ps"), sem("k_rot_ready"), sem("kpeT_ps"), sem("kpeT_ready")
        qpe_ps, q_rot_ready, qpeT_ps, qpeT_ready = sem("qpe_ps"), sem("q_rot_ready"), sem("qpeT_ps"), sem("qpeT_ready")
        v_ps, v_ready = sem("v_ps"), sem("v_ready")
        qk_ps, qk_ready = sem("qk_ps"), sem("qk_ready")
        hs_ps, hmax_ready, hexp_ready, hp_ready = sem("hs_ps"), sem("hmax_ready"), sem("hexp_ready"), sem("hp_ready")
        pT_ps, pT_ready = sem("pT_ps"), sem("pT_ready")
        ho_ps, ho_hi_done, ho_ready = sem("ho_ps"), sem("ho_hi_done"), sem("ho_ready")
        wout_hi_done, wout_lo_done = sem("wout_hi_done"), sem("wout_lo_done")
        wout_used = sem("wout_used")
        x2_ready = sem("x2_ready")
        gate_ps, g_neg_ready, g_exp_ready = sem("gate_ps"), sem("g_neg_ready"), sem("g_exp_ready")
        onehot_ready, pos_ps, sel_ready = sem("onehot_ready"), sem("pos_ps"), sem("sel_ready")
        combT_ps, combT_ready = sem("combT_ps"), sem("combT_ready")
        gate_in, swd_used = sem("gate_in"), sem("swd_used")
        norm_hi, norm_lo = sem("norm_hi"), sem("norm_lo")
        raw_in = [sem(f"raw_in{s}") for s in range(RAW)]
        w_hi_done, w_lo_done, w_used = sem("w_hi_done"), sem("w_lo_done"), sem("w_used")
        wd_in, wub_in, swub_in = sem("wd_in"), sem("wub_in"), sem("swub_in")
        gather_ps, xs_hi_done, xs_ready = sem("gather_ps"), sem("xs_hi_done"), sem("xs_ready")
        adapt_ps, ga_ready, gs_ready = sem("adapt_ps"), sem("ga_ready"), sem("gs_ready")
        a_copied, a_turned = sem("a_copied"), sem("a_turned")
        gelu_done, b1e_ready = sem("gelu_done"), sem("b1e_ready")
        hid_hi_done, hid_ready = sem("hid_hi_done"), sem("hid_ready")
        sgelu_done, shid_hi_done, shid_ready = sem("sgelu_done"), sem("shid_hi_done"), sem("shid_ready")
        slot_w_ps, y_hi_done = sem("slot_w_ps"), sem("y_hi_done")
        y_ps, y_ready, ct_ready = sem("y_ps"), sem("y_ready"), sem("ct_ready")
        comb_ps, comb_added, sh_added = sem("comb_ps"), sem("comb_added"), sem("sh_added")
        out_ready, out_stored = sem("out_ready"), sem("out_stored")

        ctx_v = ctx.rearrange("(b p j) d -> b p j d", p=P, j=KJ)
        mask_rows_v = mask.rearrange("(b n) -> b n", n=HALF)
        out_v = out.rearrange("a (t p) d -> p (a t) d", p=P)

        def half_source(e, n):
            (kind, k), x = ROUND[n // 2], n % 2
            if kind == "w1":
                return w1[bass.ds(e, 1)].rearrange("a (c p) f -> p (a c) f", p=P)[:, 4 * x:4 * x + 4, k * HALF:(k + 1) * HALF]
            if kind == "w2":
                return w2[bass.ds(e, 1)].rearrange("a (k x j p) d -> k x p (a j) d", x=2, j=2, p=P)[k, x]
            if kind == "s1":
                return sw1.rearrange("(c p) (s x f) -> s x p c f", p=P, s=STEPS, x=2)[bass.ds(e, 1), x]\
                    .rearrange("a p c f -> (a p) c f")
            return sw2.rearrange("(s x j p) d -> s x p j d", x=2, j=2, p=P)[bass.ds(e, 1), x].rearrange("a p j d -> (a p) j d")

        def half_view(v, n):
            return v.rearrange("p (c f) -> p c f", c={"w1": 4, "w2": 2, "s1": 8, "s2": 2}[ROUND[n // 2][0]])

        out_sb = late_part(4096, [NT, D])
        block = stack.enter_context(nc.Block())

        @block.sync
        def _(sp):
            sp.dma_start(mask_blocks[:, :], mask_rows_v[1:1 + NBLK, :]).then_inc(mask_in, 16)
            sp.dma_start(cst[:, :], consts).then_inc(consts_in, 16)
            sp.dma_start(x_sb[:, :, :], x.rearrange("a (t p) d -> p (a t) d", p=P)).then_inc(x_in, 16)
            sp.dma_start(b1_raw[:, 0:2, :], b1.rearrange("e (f q) -> (e f) q", q=P).rearrange("(a r) q -> r a q", r=P))\
                .then_inc(small_in, 16)
            sp.dma_start(b1_raw[0:NF, 2, :], sb1.rearrange("(f q) -> f q", q=P)).then_inc(small_in, 16)
            sp.wait_ge(list_ready, 1)
            pairs = sp.value_load(pairs_i[0:1, 0:1], min_val=1, max_val=NLIST // 2)
            with sp.Fori(0, pairs) as i:
                sp.wait_ge(pair_done, i + 1)
                for b in range(2):
                    c = sp.value_load(ctx_ix[0:1, bass.ds(i * 2 + b, 1)], min_val=0, max_val=NBLK - 1)
                    m = sp.value_load(mask_ix[0:1, bass.ds(i * 2 + b, 1)], min_val=0, max_val=NBLK)
                    sp.dma_start(mask_row[0:1, b, :], mask_rows_v[bass.ds(m, 1), :]).then_inc(mrow_in[b], 16)
                    sp.dma_start(ctx_t[b], ctx_v[bass.ds(c, 1)].rearrange("b p j d -> (b p) j d")).then_inc(ctx_in[b], 16)
            sp.dma_start(wqa_sb, Wqa.rearrange("(c p) n -> p c n", p=P)).then_inc(wq_in, 16)
            sp.dma_start(wkva_sb, Wkva.rearrange("(c p) n -> p c n", p=P)).then_inc(wkv_in, 16)
            sp.dma_start(wqb_sb.rearrange("p k h n -> p k (h n)"),
                         Wqb.rearrange("(k p) n -> p k n", p=P)).then_inc(wq_in, 16)
            sp.dma_start(wkvb_sb.rearrange("p k h n -> p k (h n)"),
                         Wkvb.rearrange("(k p) n -> p k n", p=P)).then_inc(wkv_in, 16)
            sp.dma_start(gate_sb[:, :, :], gate_w.rearrange("(c p) e -> p c e", p=P)).then_inc(gate_in, 16)
            sp.wait_ge(ln_h_ready[1], 1)
            for s in range(4):
                sp.dma_start(wout_sb[:, 4 * s:4 * s + 4, :],
                             Wout[s * HALF:(s + 1) * HALF, :].rearrange("(h p) n -> p h n", p=P)).then_inc(wout_in[s], 16)
            sp.wait_ge(qk_ps, H)
            for n in range(RAW):
                sp.dma_start(half_view(raw[:, n, :], n), half_source(0, n)).then_inc(raw_in[n], 16)
            sp.wait_ge(x2_ready, NT * 2)
            sp.dma_start(wd_sb, swd.rearrange("(c p) r -> p c r", p=P)).then_inc(wd_in, 16)
            sp.dma_start(wub_sb[0:AR].rearrange("p a b -> p (a b)"), wu[0]).then_inc(wub_in, 16)
            sp.dma_start(wub_sb[AR:AR + 1].rearrange("p a b -> p (a b)"), b2[0:1, :]).then_inc(wub_in, 16)
            sp.dma_start(swub_sb[0:AR].rearrange("p a b -> p (a b)"), swu).then_inc(swub_in, 16)
            sp.dma_start(swub_sb[AR:AR + 1].rearrange("p a b -> p (a b)"), sb2.rearrange("(a d) -> a d", a=1))\
                .then_inc(swub_in, 16)
            sp.wait_ge(adapt_ps, 1)
            sp.dma_start(wd_sb, wd[0].rearrange("(c p) r -> p c r", p=P)).then_inc(wd_in, 16)

            def load(e, n, source_e, m):
                sp.wait_ge(w_lo_done, NHALF * e + n + 1)
                sp.dma_start(half_view(raw[:, m % RAW, :], m), half_source(source_e, m)).then_inc(raw_in[m % RAW], 16)

            with sp.Fori(0, E - 1) as e:
                for n in range(NHALF):
                    if n + RAW < NHALF:
                        load(e, n, e, n + RAW)
                    else:
                        load(e, n, e + 1, n + RAW - NHALF)
                    if n == 10:
                        sp.wait_ge(adapt_ps, e + 2)
                        sp.dma_start(wd_sb, wd[bass.ds(e + 1, 1)].rearrange("a (c p) r -> p (a c) r", p=P)).then_inc(wd_in, 16)
                sp.wait_ge(y_ps, e + 2)
                sp.dma_start(wub_sb[0:AR].rearrange("p a b -> p (a b)"),
                             wu[bass.ds(e + 1, 1)].rearrange("a r d -> (a r) d")).then_inc(wub_in, 16)
                sp.dma_start(wub_sb[AR:AR + 1].rearrange("p a b -> p (a b)"), b2[bass.ds(e + 1, 1), :])\
                    .then_inc(wub_in, 16)
            for n in range(NHALF - RAW):
                load(E - 1, n, E - 1, n + RAW)
            for t in range(NT):
                for a in range(2):
                    sp.wait_ge(out_ready, 2 * t + a + 1)
                    sp.dma_start(out_v[:, t, a * HALF:(a + 1) * HALF], out_sb[:, t, a * HALF:(a + 1) * HALF])\
                        .then_inc(out_stored, 16)
            sp.wait_ge(out_stored, 16 * NT * 2)

        @block.scalar
        def _(act):
            def layernorm_sd(n):
                act.wait_ge(ln_var_ready[n], 1)
                nc.scalar.activation(ln_sd[:, :], ln_var[:, :], ACT.Sqrt).then_inc(ln_sd_ready[n], 1)

            def layernorm_drain(n, scale, hT=hT):
                for t in range(NT):
                    act.wait_ge(lnT_ps[n], 2 * t + 1)
                    nc.scalar.activation(hT[:, 0:4, t * P:(t + 1) * P], ps[:, 2 * t, :].rearrange("p (c q) -> p c q", c=4),
                                         ACT.Copy, scale=scale).then_inc(lnT_act[n], 1)

            act.sem_inc(t_drained[0], 1)
            layernorm_sd(0)
            layernorm_drain(0, 1.0 / 32)
            act.wait_ge(b1_ps, 1)
            nc.scalar.activation(b1T[:, :], ps[:, 7, 0:(E + 1) * NF], ACT.Copy).then_inc(b1T_ready, 1)

            act.wait_ge(list_ready, 1)
            pairs = act.value_load(pairs_i[0:1, 0:1], min_val=1, max_val=NLIST // 2)
            with act.Fori(0, pairs) as i:
                for b in range(2):
                    for c in range(0, NC, 2):
                        act.wait_ge(t_filled[0], 10 * i + 4 * b + c // 2 + 1)
                        nc.scalar.activation(kT[b][:, c, :], ps[:, 4, :], ACT.Copy).then_inc(t_drained[0], 1)
                for q in range(NT):
                    act.wait_ge(exp_args_ready[q], 2 * i + 2)
                    nc.scalar.activation(alpha[:, q:q + 1], old_less_new[:, q:q + 1], ACT.Exp)
                    nc.scalar.activation(prob[:, q, :].rearrange("p (b k) -> p b k", b=2), ps[:, 2 * q:2 * q + 2, :], ACT.Exp,
                                         bias=neg_max[:, q:q + 1], accum_out=row_sum[:, q:q + 1]).then_inc(p_ready[q], 1)
                    act.wait_ge(t_filled[0], 10 * i + 8 + q + 1)
                    nc.scalar.activation(probT[:, q, 0:HALF], ps[:, 4, :], ACT.Copy).then_inc(t_drained[0], 1)

            layernorm_sd(1)
            layernorm_drain(1, 1.0)
            act.wait_ge(proj_ps, 1)
            nc.scalar.activation(qaT, ps[:, 4, :].rearrange("p (k t) -> p k t", k=NR), ACT.Copy).then_inc(qaT_ready, 1)
            def queries_turned(t):
                act.wait_ge(qpeT_ps, t + 1)
                nc.scalar.activation(q_peT[:, :, t * P:(t + 1) * P],
                                     ps[:, 2 * t:2 * t + 2, :].rearrange("p b (h q) -> p (b h) q", h=4), ACT.Copy)\
                    .then_inc(qpeT_ready, 1)

            for n in range(2 * NT * 2):
                act.wait_ge(v_ps, n + 1)
                nc.scalar.activation(v_sb[:, n // 4, 4 * (n % 4):4 * (n % 4) + 4, :],
                                     ps[:, 4 + n % 2, :].rearrange("p (h v) -> p h v", h=4), ACT.Copy).then_inc(v_ready, 1)
                if n == TURN:
                    act.wait_ge(kpeT_ps, 1)
                    nc.scalar.activation(k_peT, ps[:, 7, 0:TOK], ACT.Copy).then_inc(kpeT_ready, 1)
                    queries_turned(0)
            for s in range(H + 4):
                if s == 1:
                    queries_turned(1)
                if s < H:
                    act.wait_ge(qk_ps, s + 1)
                    nc.scalar.activation(qkT[:, s % 2, :], ps[:, 4, :], ACT.Copy).then_inc(qk_ready, 1)
                if 0 <= s - 1 < H:
                    g = s - 1
                    act.wait_ge(hmax_ready, g + 1)
                    nc.scalar.activation(p_sb[:, g % 2, 0, :], ps[:, 5, 0:P], ACT.Exp, bias=s_bias[:, g % 2, 0:1],
                                         scale=SCALE, accum_out=s_sum[:, g % 2, 0:1])
                    nc.scalar.activation(p_sb[:, g % 2, 1:3, :], ps[:, 5, P:3 * P].rearrange("p (a k) -> p a k", a=2), ACT.Exp,
                                         bias=s_bias[:, g % 2, 1:2], scale=SCALE, accum_out=s_sum[:, g % 2, 1:2])\
                        .then_inc(hexp_ready, 1)
                if 0 <= s - 3 < H:
                    g = s - 3
                    act.wait_ge(ho_ps, g + 1)
                    if g >= 2:
                        act.wait_ge(wout_used, g - 1)
                    nc.scalar.activation(attn_s[0][:, g % 2, :], ps[:, 7, 0:TOK], ACT.Copy).then_inc(ho_hi_done, 1)
                    if g % 4 == 0:
                        act.wait_ge(wout_in[g // 4], 16)
                    nc.scalar.activation(wout_s[0][:, g % 2, :], wout_sb[:, g, :], ACT.Copy).then_inc(wout_hi_done, 1)

            def gathered_hi(count):
                act.wait_ge(gather_ps, count)
                nc.scalar.activation(xs_s[0][:, :, :].rearrange("p (a c) s -> p a (c s)", a=2), ps[:, 0:2, 0:4 * SLOTS],
                                     ACT.Copy).then_inc(xs_hi_done, 1)
                nc.scalar.activation(xs.rearrange("p (a c) s -> p a (c s)", a=2), ps[:, 0:2, 0:4 * SLOTS], ACT.Copy)\
                    .then_inc(xs_hi_done, 1)

            def weigh_hi(count):
                act.wait_ge(y_ps, count)
                act.wait_ge(ct_ready, count)
                nc.scalar.activation(y_s[0][:, :, :], ps[0:SLOTS, 3:5, :], ACT.Copy, scale=slot_w_e[:, 0:1]).then_inc(y_hi_done, 1)

            def half(e, n):
                at = NHALF * e + n
                act.wait_ge(raw_in[n % RAW], 16 * (NHALF // RAW * e + n // RAW + 1))
                act.wait_ge(w_used, at + 1)
                nc.scalar.activation(w_s[0][:, n % SPLIT, :], raw[:, n % RAW, :], ACT.Copy).then_inc(w_hi_done, 1)
                if n == 3:
                    act.wait_ge(w_used, NHALF * e + 2 + SPLIT)
                    act.wait_ge(b1e_ready, e + 1)
                    for j in range(4):
                        last = nc.scalar.activation(shid[:, j, :], ps[:, 5 + j // 2, (j % 2) * TOK:(j % 2 + 1) * TOK],
                                                    ACT.Gelu, bias=b1_e[:, NF + j:NF + j + 1])
                    last.then_inc(sgelu_done, 1)
                if n == 4:
                    act.wait_ge(adapt_ps, e + 2)
                    nc.scalar.activation(ga[0:AR, :], ps[0:AR, 7, 0:SLOTS], ACT.Gelu).then_inc(ga_ready, 1)
                if n == 5:
                    act.wait_ge(sgelu_done, e + 1)
                    nc.scalar.activation(shid_s[0][:, :, :], shid, ACT.Copy).then_inc(shid_hi_done, 1)
                for k in range(STEPS):
                    first = FIRST_HALF["w1", k]
                    if n == first + 3:
                        act.wait_ge(w_used, NHALF * e + first + 2 + SPLIT)
                        nc.scalar.activation(a_sb, ps[0:SLOTS, k % 2, :], ACT.Copy).then_inc(a_copied, 1)
                    if n == first + 4:
                        act.wait_ge(a_turned, STEPS * e + k + 1)
                        for j in range(4):
                            last = nc.scalar.activation(hid[:, j, :], ps[:, 2, j * SLOTS:(j + 1) * SLOTS], ACT.Gelu,
                                                        bias=b1_e[:, 4 * k + j:4 * k + j + 1])
                        last.then_inc(gelu_done, 1)

            layernorm_sd(2)
            layernorm_drain(2, 1.0, fT)
            act.wait_ge(lnT_act[2], NT)
            act.wait_ge(lnT_dve[2], NT)
            for t in range(NT):
                nc.scalar.activation(hT_s[0][:, :, t * P:(t + 1) * P], fT[:, :, t * P:(t + 1) * P], ACT.Copy)\
                    .then_inc(norm_hi, 1)
            act.sem_inc(gelu_done, 1)
            half(0, 0)
            half(0, 1)
            act.wait_ge(g_neg_ready, 1)
            for t in range(NT):
                nc.scalar.activation(g_exp[:, t, :], ps[:, 4, t * E:(t + 1) * E], ACT.Exp, bias=g_neg[:, t:t + 1],
                                     accum_out=g_sum[:, t:t + 1]).then_inc(g_exp_ready, 1)
            act.wait_ge(adapt_ps, 1)
            nc.scalar.activation(gs[0:AR, :], ps[0:AR, 7, 0:TOK], ACT.Gelu).then_inc(gs_ready, 1)
            half(0, 2)
            gathered_hi(1)
            act.wait_ge(norm_lo, NT)
            for n in range(4):
                bank = COMB_BANKS[n]
                act.wait_ge(combT_ps, n + 1)
                nc.scalar.activation(combT[:, 2 * n:2 * n + 2, :],
                                     ps[0:SLOTS, bank, :].rearrange("p (e t) -> p e t", e=2), ACT.Copy).then_inc(combT_ready, 1)
            act.wait_ge(slot_w_ps, 1)
            with act.Fori(0, E - 1) as e:
                for n in range(SPLIT, NHALF):
                    half(e, n)
                for n in range(SPLIT):
                    half(e + 1, n)
                weigh_hi(e + 2)
                gathered_hi(e + 2)
            for n in range(SPLIT, NHALF):
                half(E - 1, n)
            weigh_hi(E + 1)

        @block.vector
        def _(dve):
            chain = [0]

            def link(ins):
                chain[0] += 1
                ins.then_inc(dve_chain, 1)
                dve.wait_ge(dve_chain, chain[0])

            def layernorm(n, hN=hN):
                for t in range(NT):
                    for a in range(2):
                        last = nc.vector.bn_stats(ln_st[:, t, a, :], x_sb[:, t, a * HALF:(a + 1) * HALF])
                link(last)
                for t in range(NT):
                    last = nc.vector.bn_aggr(ln_mv[:, t, :], ln_st[:, t, :, :].rearrange("p a s -> p (a s)"))
                link(last)
                nc.vector.tensor_scalar(ln_var[:, :], ln_mv[:, :, 1], EPS, None, ALU.add).then_inc(ln_var_ready[n], 1)
                dve.wait_ge(ln_sd_ready[n], 1)
                link(nc.vector.reciprocal(ln_rs[:, :], ln_sd[:, :]))
                for t in range(NT):
                    nc.vector.tensor_scalar(hN[:, t, :], x_sb[:, t, :], ln_mv[:, t, 0:1], ln_rs[:, t:t + 1],
                                            ALU.subtract, ALU.mult).then_inc(ln_h_ready[n], 1)

            def layernorm_drain(n, scale, hT=hT):
                for t in range(NT):
                    dve.wait_ge(lnT_ps[n], 2 * t + 2)
                    nc.vector.tensor_scalar(hT[:, 4:8, t * P:(t + 1) * P],
                                            ps[:, 2 * t + 1, :].rearrange("p (c q) -> p c q", c=4),
                                            scale, None, ALU.mult).then_inc(lnT_dve[n], 1)

            nc.vector.memset(onesf[:, :], 1.0).then_inc(ones_set, 1)
            nc.vector.memset(onesb[:, :], 1.0).then_inc(ones_set, 1)
            link(nc.vector.memset(work[:, :], -1.0))
            nc.vector.memset(o_acc, 0.0)
            dve.wait_ge(mask_in, 16)
            nc.vector.tensor_reduce(any_blk[:, :], mask_blocks[:, :], X, ALU.max).then_inc(any_ready, 1)
            dve.wait_ge(consts_in, 16)
            nc.vector.tensor_copy(identb[:, :], ident).then_inc(constb_set, 1)
            nc.vector.tensor_copy(upperb[:, :], cst[:, C_UP:C_UP + P]).then_inc(constb_set, 1)
            nc.vector.tensor_copy(causalb[:, :], cst[:, C_CAUS:C_CAUS + P]).then_inc(constb_set, 1)
            dve.wait_ge(any_ps, 1)
            nc.vector.tensor_scalar(valid[:, :], ps[:, 6, 64:65], 1.0, None, ALU.min)
            link(nc.vector.tensor_copy(work[:, 0:NBLK], ps[0:1, 6, 0:NBLK]))
            for r in range(NLIST // 8):
                src, dst = (work, work2) if r % 2 == 0 else (work2, work)
                link(nc.vector.max(order[:, 8 * r:8 * r + 8], src[:, :]))
                link(nc.vector.match_replace(dst[:, :], order[:, 8 * r:8 * r + 8], src[:, :], -1.0))
            nc.vector.tensor_scalar(pair_on[:, :], order[:, 0:NLIST:2], 0.0, None, ALU.is_gt)
            nc.vector.tensor_scalar(mask_ix[:, :], order[:, :], 0.0, None, ALU.max)
            link(nc.vector.tensor_scalar(ctx_ix[:, :], order[:, :], 1.0, 0.0, ALU.subtract, ALU.max))
            link(nc.vector.tensor_reduce(pairs_f[:, :], pair_on[:, :], X, ALU.add))
            nc.vector.tensor_scalar(pairs_i[:, :], pairs_f[:, :], 1.0, None, ALU.max).then_inc(list_ready, 1)

            nc.vector.memset(run_max[:, :], -3e38)
            nc.vector.memset(run_sum[:, :], 0.0)
            dve.wait_ge(x_in, 16)
            layernorm(0)
            layernorm_drain(0, 1.0 / 32)
            for b in (t_drained[1], o_added[0], o_added[1]):
                dve.sem_inc(b, 1)

            pairs = dve.value_load(pairs_i[0:1, 0:1], min_val=1, max_val=NLIST // 2)
            with dve.Fori(0, pairs) as i:
                for b in range(2):
                    dve.wait_ge(mrow_in[b], 16 * i + 16)
                    nc.vector.tensor_scalar(bias_row[0:1, b, :].rearrange("o (j p) -> o j p", j=KJ),
                                            mask_row[0:1, b, :].rearrange("o (p j) -> o j p", j=KJ),
                                            -NEG, NEG, ALU.mult, ALU.add).then_inc(bias_ready, 1)
                for b in range(2):
                    for c in range(1, NC, 2):
                        dve.wait_ge(t_filled[1], 10 * i + 4 * b + c // 2 + 1)
                        nc.vector.tensor_copy(kT[b][:, c, :], ps[:, 5, :]).then_inc(t_drained[1], 1)
                for q in range(NT):
                    one = slice(q, q + 1)
                    dve.wait_ge(s_ready[q], i + 1)
                    nc.vector.tensor_reduce(blk_max[:, one], ps[:, 2 * q:2 * q + 2, :], mybir.AxisListType.XY, ALU.max)\
                        .then_inc(blk_max_ready[q], 1)
                    dve.wait_ge(blk_max_ready[q], i + 1)
                    nc.vector.tensor_tensor(new_max[:, one], run_max[:, one], blk_max[:, one], ALU.max)\
                        .then_inc(new_max_ready[q], 1)
                    dve.wait_ge(new_max_ready[q], i + 1)
                    nc.vector.tensor_scalar(neg_max[:, one], new_max[:, one], -1.0, None, ALU.mult)\
                        .then_inc(exp_args_ready[q], 1)
                    nc.vector.tensor_tensor(old_less_new[:, one], run_max[:, one], new_max[:, one], ALU.subtract)\
                        .then_inc(exp_args_ready[q], 1)
                for q in range(NT):
                    dve.wait_ge(t_filled[1], 10 * i + 8 + q + 1)
                    nc.vector.tensor_copy(probT[:, q, HALF:2 * HALF], ps[:, 5, :]).then_inc(t_drained[1], 1)
                for q in range(NT):
                    one = slice(q, q + 1)
                    dve.wait_ge(p_ready[q], i + 1)
                    nc.vector.scalar_tensor_tensor(out=run_sum[:, one], in0=run_sum[:, one], scalar=alpha[:, one],
                                                   in1=row_sum[:, one], op0=ALU.mult, op1=ALU.add)
                    nc.vector.tensor_copy(run_max[:, one], new_max[:, one])
                    dve.wait_ge(pv_ready[q], i + 1)
                    acc = o_acc[:, q, :].rearrange("p (a d) -> p a d", a=2)
                    bank = 6 if q == 0 else 0
                    nc.vector.scalar_tensor_tensor(out=acc, in0=acc, scalar=alpha[:, one], in1=ps[:, bank:bank + 2, :],
                                                   op0=ALU.mult, op1=ALU.add).then_inc(o_added[q], 1)
            for q in range(NT):
                dve.wait_ge(o_added[q], pairs + 1)
            link(nc.vector.reciprocal(inv_sum[:, :], run_sum[:, :]))
            link(nc.vector.tensor_scalar(inv_valid[:, :], inv_sum[:, :], valid[:, 0:1], None, ALU.mult))
            for t in range(NT):
                last = nc.vector.scalar_tensor_tensor(out=x_sb[:, t, :], in0=o_acc[:, t, :], scalar=inv_valid[:, t:t + 1],
                                                      in1=x_sb[:, t, :], op0=ALU.mult, op1=ALU.add)
            link(last)

            layernorm(1)
            layernorm_drain(1, 1.0)
            dve.wait_ge(proj_ps, 2)
            nc.vector.tensor_copy(compT, ps[:, 5, :].rearrange("p (k t) -> p k t", k=NR)).then_inc(compT_ready, 1)

            def rotate(out_even, out_odd, even, odd, cosv, sinv, shape):
                n = shape[0] * shape[1]
                tmp = [rope_tmp[:, k, 0:n].rearrange("p (a b) -> p a b", a=shape[0]) for k in range(4)]
                nc.vector.tensor_tensor(tmp[0], even, cosv, ALU.mult)
                nc.vector.tensor_tensor(tmp[1], odd, sinv, ALU.mult)
                nc.vector.tensor_tensor(tmp[2], even, sinv, ALU.mult)
                link(nc.vector.tensor_tensor(tmp[3], odd, cosv, ALU.mult))
                nc.vector.tensor_tensor(out_even, tmp[0], tmp[1], ALU.subtract)
                return nc.vector.tensor_tensor(out_odd, tmp[2], tmp[3], ALU.add)

            dve.wait_ge(kpe_ps, 1)
            kv = ps[:, 6, 0:NT * ROPE].rearrange("p (t i two) -> p t i two", t=NT, two=2)
            kr = k_rot.rearrange("p t u (i two) -> p t u i two", two=2)
            link(rotate(kr[:, :, 0, :, 0], kr[:, :, 0, :, 1], kv[:, :, :, 0], kv[:, :, :, 1], cos, sin, [NT, 32]))
            nc.vector.tensor_copy(k_rot[:, :, 1, :], k_rot[:, :, 0, :]).then_inc(k_rot_ready, 1)
            for t in range(NT):
                for a in range(2):
                    dve.wait_ge(qpe_ps, 2 * t + a + 1)
                    if t > 0:
                        dve.wait_ge(qpeT_ps, t)
                    if t + a > 0:
                        dve.wait_ge(q_rot_ready, 2 * t + a)
                    qv = ps[:, 2 * t + a, :].rearrange("p (h i two) -> p h i two", h=8, two=2)
                    qr = q_rot[:, 8 * a:8 * a + 8, :].rearrange("p h (i two) -> p h i two", two=2)
                    cosb = cos[:, t, :].unsqueeze(1).broadcast_to([P, 8, 32])
                    sinb = sin[:, t, :].unsqueeze(1).broadcast_to([P, 8, 32])
                    rotate(qr[:, :, :, 0], qr[:, :, :, 1], qv[:, :, :, 0], qv[:, :, :, 1], cosb, sinb, [8, 32])\
                        .then_inc(q_rot_ready, 1)
            for s in range(H + 4):
                if 0 <= s - 1 < H:
                    g = s - 1
                    dve.wait_ge(hs_ps, g + 1)
                    nc.vector.tensor_reduce(s_max[:, g % 2, 0:1], ps[:, 5, 0:P], X, ALU.max)
                    link(nc.vector.tensor_reduce(s_max[:, g % 2, 1:2], ps[:, 5, P:3 * P], X, ALU.max))
                    nc.vector.tensor_scalar(s_bias[:, g % 2, :], s_max[:, g % 2, :], -SCALE, None, ALU.mult)\
                        .then_inc(hmax_ready, 1)
                    dve.wait_ge(hexp_ready, g + 1)
                    link(nc.vector.reciprocal(s_inv[:, g % 2, :], s_sum[:, g % 2, :]))
                    nc.vector.tensor_scalar(p_sb[:, g % 2, 0, :], p_sb[:, g % 2, 0, :], s_inv[:, g % 2, 0:1], None, ALU.mult)
                    nc.vector.tensor_scalar(p_sb[:, g % 2, 1:3, :], p_sb[:, g % 2, 1:3, :], s_inv[:, g % 2, 1:2], None,
                                            ALU.mult).then_inc(hp_ready, 1)
                if 0 <= s - 2 < H:
                    g = s - 2
                    dve.wait_ge(pT_ps, g + 1)
                    nc.vector.tensor_copy(pT_sb[:, g % 2, :, :], ps[:, 6, 0:3 * P].rearrange("p (a k) -> p a k", a=3))\
                        .then_inc(pT_ready, 1)
                if 0 <= s - 3 < H:
                    g = s - 3
                    dve.wait_ge(ho_hi_done, g + 1)
                    nc.vector.tensor_tensor(attn_s[1][:, g % 2, :], ps[:, 7, 0:TOK], attn_s[0][:, g % 2, :].bitcast(F32),
                                            ALU.subtract).then_inc(ho_ready, 1)
                    dve.wait_ge(wout_hi_done, g + 1)
                    nc.vector.tensor_tensor(wout_s[1][:, g % 2, :], wout_sb[:, g, :], wout_s[0][:, g % 2, :].bitcast(F32),
                                            ALU.subtract).then_inc(wout_lo_done, 1)
            dve.wait_ge(wout_used, H)
            for t in range(NT):
                for a in range(2):
                    xs = x_sb[:, t, a * HALF:(a + 1) * HALF]
                    last = nc.vector.tensor_tensor(xs, xs, ps[:, 2 * t + a, :], ALU.add)
                    last.then_inc(x2_ready, 1)
            dve.wait_ge(x2_ready, NT * 2)

            def gathered_lo(count):
                dve.wait_ge(xs_hi_done, 2 * count)
                nc.vector.tensor_tensor(xs_s[1][:, :, :].rearrange("p (a c) s -> p a (c s)", a=2), ps[:, 0:2, 0:4 * SLOTS],
                                        xs_s[0][:, :, :].bitcast(F32).rearrange("p (a c) s -> p a (c s)", a=2), ALU.subtract)\
                    .then_inc(xs_ready, 1)

            def weigh_lo(count):
                dve.wait_ge(y_hi_done, count)
                nc.vector.scalar_tensor_tensor(out=y_s[1][:, :, :], in0=ps[0:SLOTS, 3:5, :], scalar=slot_w_e[:, 0:1],
                                               in1=y_s[0][:, :, :].bitcast(F32), op0=ALU.mult, op1=ALU.subtract).then_inc(y_ready, 1)

            def add_expert(e, rows):
                for r in rows:
                    dve.wait_ge(comb_ps, 4 * e + r + 1)
                    to = x_sb[:, r // 2, (r % 2) * HALF:(r % 2 + 1) * HALF]
                    nc.vector.tensor_tensor(to, to, ps[:, (5, 6, 7, 5)[r], :], ALU.add).then_inc(comb_added, 1)

            def half(e, n):
                at = NHALF * e + n
                dve.wait_ge(w_hi_done, at + 1)
                nc.vector.tensor_tensor(w_s[1][:, n % SPLIT, :], raw[:, n % RAW, :], w_s[0][:, n % SPLIT, :].bitcast(F32),
                                        ALU.subtract).then_inc(w_lo_done, 1)
                if n == 0:
                    dve.wait_ge(gelu_done, STEPS * e + 1)
                    nc.vector.tensor_copy(b1_e[:, 0:NF], b1T[:, bass.ds(e * NF, NF)])
                    nc.vector.tensor_copy(b1_e[:, NF:NF + 4], b1T[:, bass.ds(e * 4 + E * NF, 4)]).then_inc(b1e_ready, 1)
                for k in range(STEPS):
                    if n == FIRST_HALF["w1", k] + 4:
                        dve.wait_ge(gelu_done, STEPS * e + k + 2)
                        nc.vector.tensor_copy(hid_s[0][:, k % 2, :, :], hid).then_inc(hid_hi_done, 1)
                        dve.wait_ge(hid_hi_done, STEPS * e + k + 1)
                        nc.vector.tensor_tensor(hid_s[1][:, k % 2, :, :], hid, hid_s[0][:, k % 2, :, :].bitcast(F32),
                                                ALU.subtract).then_inc(hid_ready, 1)
                if n in (7, 9):
                    dve.wait_ge(shid_hi_done, e + 1)
                    two = slice(n - 7, n - 5)
                    nc.vector.tensor_tensor(shid_s[1][:, two, :], shid[:, two, :], shid_s[0][:, two, :].bitcast(F32),
                                            ALU.subtract).then_inc(shid_ready, 1)
                if n == COMBINE + 2:
                    add_expert(e, (0, 1, 2))
                if n == COMBINE + 5:
                    add_expert(e, (3,))
                    nc.vector.tensor_copy(slot_w_e[:, :], slot_w[:, bass.ds(e, 1)])
                    nc.vector.tensor_copy(ct_e[:, :], combT[:, bass.ds(e, 1), :].rearrange("p a t -> p (a t)"))\
                        .then_inc(ct_ready, 1)

            def add_shared(e):
                dve.wait_ge(w_used, NHALF * e + FIRST_HALF["s2", 0] + 2 + SPLIT)
                for r in range(2 * NT):
                    to = x_sb[:, r // 2, (r % 2) * HALF:(r % 2 + 1) * HALF]
                    nc.vector.scalar_tensor_tensor(out=to, in0=ps[:, S_BANKS[r], :], scalar=0.2, in1=to,
                                                   op0=ALU.mult, op1=ALU.add).then_inc(sh_added, 1)

            layernorm(2, fN)
            nc.vector.memset(ga[AR:AR + 1, :], 1.0)
            nc.vector.memset(gs[AR:AR + 1, :], 1.0)
            nc.vector.memset(ct_e[:, :].bitcast(F32), 0.0)
            for y in y_s:
                nc.vector.memset(y[:, :, :].bitcast(F32), 0.0)
            layernorm_drain(2, 1.0, fT)
            dve.wait_ge(norm_hi, NT)
            for t in range(NT):
                at = (slice(None), slice(None), slice(t * P, (t + 1) * P))
                nc.vector.tensor_tensor(hT_s[1][at], fT[at], hT_s[0][at].bitcast(F32), ALU.subtract).then_inc(norm_lo, 1)
            dve.wait_ge(b1T_ready, 1)
            half(0, 0)
            dve.wait_ge(gate_ps, 1)
            link(nc.vector.tensor_reduce(g_max[:, :], ps[:, 4, 0:NT * E].rearrange("p (t e) -> p t e", t=NT), X, ALU.max))
            nc.vector.tensor_scalar(g_neg[:, :], g_max[:, :], -1.0, None, ALU.mult).then_inc(g_neg_ready, 1)
            dve.wait_ge(g_exp_ready, NT)
            link(nc.vector.reciprocal(g_inv[:, :], g_sum[:, :]))
            for t in range(NT):
                last = nc.vector.tensor_scalar(probs[:, t, :], g_exp[:, t, :], g_inv[:, t:t + 1], None, ALU.mult)
            link(last)
            for t in range(NT):
                last = nc.vector.max(top_v[:, t, :], probs[:, t, :])
            link(last)
            for t in range(NT):
                last = nc.vector.max_index(top_i[:, t, :], top_v[:, t, :], probs[:, t, :])
            link(last)
            link(nc.vector.tensor_copy(top_f[:, :, :], top_i[:, :, :]))
            for t in range(NT):
                for k in range(TOPK):
                    last = nc.vector.tensor_scalar(onehot[:, t, :, k], cst[:, C_I8:C_I8 + E], top_f[:, t, k:k + 1], None,
                                                   ALU.is_equal)
            link(last)
            flat = onehot[:, :, :, :].rearrange("p t e k -> p t (e k)")
            nc.vector.tensor_copy(onehotb[:, :, :], flat).then_inc(onehot_ready, 1)
            link(nc.vector.tensor_scalar(far[:, :, :], flat, -1000.0, 1000.0, ALU.mult, ALU.add))
            half(0, 1)
            half(0, 2)
            dve.wait_ge(pos_ps, 1)
            link(nc.vector.tensor_tensor(slot[:, :, :], far[:, :, :],
                                         ps[:, 2, 0:NT * E * TOPK].rearrange("p (t n) -> p t n", t=NT), ALU.add))
            for t in range(NT):
                last = nc.vector.tensor_tensor(sel[:, t, :].rearrange("p (n s) -> p n s", s=CAP),
                                               cst[:, C_I40:C_I40 + CAP].unsqueeze(1).broadcast_to([P, E * TOPK, CAP]),
                                               slot[:, t, :].unsqueeze(2).broadcast_to([P, E * TOPK, CAP]), ALU.is_equal)
            link(last)
            for t in range(NT):
                for k in range(TOPK):
                    one = [v.rearrange("p (e k s) -> p e k s", e=E, k=TOPK)[:, :, k, :]
                           for v in (sel[:, t, :], selw[:, t, :])]
                    nc.vector.tensor_scalar(one[1], one[0], top_v[:, t, k:k + 1], None, ALU.mult).then_inc(sel_ready, 1)

            gathered_lo(1)
            dve.wait_ge(combT_ready, 4)
            dve.wait_ge(slot_w_ps, 1)
            nc.vector.tensor_copy(slot_w[:, :], ps[0:SLOTS, 4, 0:E])
            for s in (y_ps, y_hi_done, y_ready):
                dve.sem_inc(s, 1)
            dve.sem_inc(ct_ready, 1)
            dve.sem_inc(sh_added, 1)

            with dve.Fori(0, E - 1) as e:
                for n in range(SPLIT, NHALF):
                    half(e, n)
                add_shared(e)
                for n in range(SPLIT):
                    half(e + 1, n)
                weigh_lo(e + 2)
                gathered_lo(e + 2)
            for n in range(SPLIT, NHALF):
                half(E - 1, n)
            add_shared(E - 1)
            weigh_lo(E + 1)
            for r in range(2 * NT):
                t, a = r // 2, r % 2
                dve.wait_ge(comb_ps, 4 * E + r + 1)
                nc.vector.tensor_tensor(out_sb[:, t, a * HALF:(a + 1) * HALF], x_sb[:, t, a * HALF:(a + 1) * HALF],
                                        ps[:, S_BANKS[r], :], ALU.add).then_inc(out_ready, 1)

        @block.tensor
        def _(pe):
            mm, turn = nc.tensor.matmul, nc.tensor.transpose

            def layernorm_turn(n, hN=hN):
                for t in range(NT):
                    pe.wait_ge(ln_h_ready[n], t + 1)
                    for a in range(2):
                        for c in range(4):
                            cc = 4 * a + c
                            last = turn(ps[:, 2 * t + a, c * P:(c + 1) * P], hN[:, t, cc * P:(cc + 1) * P], ident)
                        last.then_inc(lnT_ps[n], 1)
                pe.wait_ge(lnT_act[n], NT)
                pe.wait_ge(lnT_dve[n], NT)

            pe.sem_inc(pair_done, 1)
            pe.wait_ge(consts_in, 16)
            pe.wait_ge(ones_set, 2)
            pe.wait_ge(any_ready, 1)
            mm(ps[0:1, 6, 0:NBLK], any_blk[:, :], cst[0:NBLK, C_BNO:C_BNO + NBLK], start=True, stop=True)
            mm(ps[:, 6, 64:65], onesf[0:NBLK, :], any_blk[:, :], start=True, stop=True).then_inc(any_ps, 1)
            layernorm_turn(0)
            pe.wait_ge(small_in, 32)
            for a in range(2):
                turn(ps[:, 7, a * P:(a + 1) * P], b1_raw[:, a, :], ident)
            turn(ps[:, 7, 2 * P:2 * P + NF], b1_raw[0:NF, 2, :], ident[0:NF, 0:NF]).then_inc(b1_ps, 1)
            pe.wait_ge(b1T_ready, 1)

            pe.wait_ge(list_ready, 1)
            pairs = pe.value_load(pairs_i[0:1, 0:1], min_val=1, max_val=NLIST // 2)
            with pe.Fori(0, pairs) as i:
                def turn_keys(b, c):
                    if c == 0:
                        pe.wait_ge(ctx_in[b], 16 * i + 16)
                    pe.wait_ge(t_drained[c % 2], 10 * i + 4 * b + c // 2 + 1)
                    for j in range(KJ):
                        last = turn(ps[:, 4 + c % 2, j * P:(j + 1) * P], ctx_t[b][:, j, c * P:(c + 1) * P], ident)
                    last.then_inc(t_filled[c % 2], 1)

                def score(b, c):
                    pe.wait_ge(t_drained[c % 2], 10 * i + 4 * b + c // 2 + 2)
                    for q in range(NT):
                        mm(ps[:, 2 * q + b, :], hT[:, c, q * P:(q + 1) * P], kT[b][:, c, :], start=(c == 0), stop=False)

                pe.wait_ge(o_added[1], i + 1)
                for b in range(2):
                    turn_keys(b, 0)
                    turn_keys(b, 1)
                    for c in range(NC):
                        score(b, c)
                        if c + 2 < NC:
                            turn_keys(b, c + 2)
                pe.wait_ge(bias_ready, 2 * i + 2)
                for q in range(NT):
                    for b in range(2):
                        last = mm(ps[:, 2 * q + b, :], onesb[0:1, :], bias_row[0:1, b, :], start=False, stop=True)
                    last.then_inc(s_ready[q], 1)
                for q in range(NT):
                    pe.wait_ge(p_ready[q], i + 1)
                    for b in range(2):
                        pe.wait_ge(t_drained[b], 10 * i + 8 + q + 1)
                        for j in range(KJ):
                            last = turn(ps[:, 4 + b, j * P:(j + 1) * P], prob[:, q, (KJ * b + j) * P:(KJ * b + j + 1) * P], ident)
                        last.then_inc(t_filled[b], 1)
                    if q == 0:
                        pe.wait_ge(o_added[0], i + 1)
                    bank = 6 if q == 0 else 0
                    for b in range(2):
                        pe.wait_ge(t_drained[b], 10 * i + 8 + q + 2)
                        for j in range(KJ):
                            for a in range(2):
                                last = mm(ps[:, bank + a, :], probT[:, q, (KJ * b + j) * P:(KJ * b + j + 1) * P],
                                          ctx_t[b][:, j, a * HALF:(a + 1) * HALF],
                                          start=(b == 0 and j == 0), stop=(b == 1 and j == KJ - 1))
                    last.then_inc(pv_ready[q], 1)
                pe.wait_ge(pv_ready[1], i + 1)
                pe.sem_inc(pair_done, 1)

            layernorm_turn(1)
            pe.wait_ge(wq_in, 32)
            for m in range(NR):
                for c in range(NC):
                    last = mm(ps[:, 4, m * TOK:(m + 1) * TOK], wqa_sb[:, c, m * P:(m + 1) * P], hT[:, c, :],
                              start=(c == 0), stop=(c == NC - 1))
            last.then_inc(proj_ps, 1)
            pe.wait_ge(wkv_in, 32)
            for m in range(NR):
                for c in range(NC):
                    last = mm(ps[:, 5, m * TOK:(m + 1) * TOK], wkva_sb[:, c, m * P:(m + 1) * P], hT[:, c, :],
                              start=(c == 0), stop=(c == NC - 1))
            last.then_inc(proj_ps, 1)
            for t in range(NT):
                for c in range(NC):
                    last = mm(ps[:, 6, t * ROPE:(t + 1) * ROPE], hT[:, c, t * P:(t + 1) * P], wkva_sb[:, c, RANK:RANK + ROPE],
                              start=(c == 0), stop=(c == NC - 1))
            last.then_inc(kpe_ps, 1)
            pe.wait_ge(qaT_ready, 1)
            for t in range(NT):
                for a in range(2):
                    for k in range(NR):
                        last = mm(ps[:, 2 * t + a, :].rearrange("p (h n) -> p h n", h=8), qaT[:, k, t * P:(t + 1) * P],
                                  wqb_sb[:, k, 8 * a:8 * a + 8, NOPE:QH], start=(k == 0), stop=(k == NR - 1))
                    last.then_inc(qpe_ps, 1)
            def turn_queries(t):
                pe.wait_ge(q_rot_ready, 2 * t + 2)
                for m in range(H // 2):
                    last = turn(ps[:, 2 * t + m // 4, (m % 4) * P:(m % 4 + 1) * P],
                                q_rot[:, 2 * m:2 * m + 2, :].rearrange("p h n -> p (h n)"), ident)
                last.then_inc(qpeT_ps, 1)

            pe.wait_ge(compT_ready, 1)
            for n in range(2 * NT * 2):
                if n >= 2:
                    pe.wait_ge(v_ready, n - 1)
                for k in range(NR):
                    last = mm(ps[:, 4 + n % 2, :].rearrange("p (h v) -> p h v", h=4), compT[:, k, (n // 4) * P:(n // 4 + 1) * P],
                              wkvb_sb[:, k, 4 * (n % 4):4 * (n % 4) + 4, NOPE:2 * NOPE], start=(k == 0), stop=(k == NR - 1))
                last.then_inc(v_ps, 1)
                if n == TURN:
                    pe.wait_ge(k_rot_ready, 1)
                    for t in range(NT):
                        last = turn(ps[:, 7, t * P:(t + 1) * P], k_rot[:, t, :, :].rearrange("p u n -> p (u n)"), ident)
                    last.then_inc(kpeT_ps, 1)
                    turn_queries(0)
            pe.wait_ge(v_ready, 2 * NT * 2)
            pe.wait_ge(constb_set, 3)

            def head_project(g):
                if g >= 1:
                    pe.wait_ge(qk_ready, g)
                for k in range(NR):
                    mm(ps[:, 4, 0:TOK], wqb_sb[:, k, g, 0:NOPE], qaT[:, k, :], start=(k == 0), stop=(k == NR - 1))
                for k in range(NR):
                    last = mm(ps[:, 4, TOK:2 * TOK], wkvb_sb[:, k, g, 0:NOPE], compT[:, k, :],
                              start=(k == 0), stop=(k == NR - 1))
                last.then_inc(qk_ps, 1)

            def head_scores(g):
                pe.wait_ge(qk_ready, g + 1)
                if g >= 1:
                    pe.wait_ge(hexp_ready, g)
                r = slice(ROPE * (g % 2), ROPE * (g % 2) + ROPE)
                for t in range(NT):
                    to, keys = ps[:, 5, t * P:(2 * t + 1) * P], (t + 1) * P
                    mm(to, qkT[:, g % 2, t * P:(t + 1) * P], qkT[:, g % 2, TOK:TOK + keys], start=True, stop=False)
                    mm(to, q_peT[r, g // 2, t * P:(t + 1) * P], k_peT[r, 0:keys], start=False, stop=False)
                    last = mm(ps[:, 5, 2 * t * P:(2 * t + 1) * P], identb[:, :], causalb[:, :], start=False, stop=True)
                last.then_inc(hs_ps, 1)

            def head_turn(g):
                pe.wait_ge(hp_ready, g + 1)
                if g >= 1:
                    pe.wait_ge(pT_ready, g)
                for m in range(3):
                    last = turn(ps[:, 6, m * P:(m + 1) * P], p_sb[:, g % 2, m, :], ident)
                last.then_inc(pT_ps, 1)

            def head_values(g):
                pe.wait_ge(pT_ready, g + 1)
                if g >= 1:
                    pe.wait_ge(ho_ready, g)
                mm(ps[:, 7, 0:TOK], v_sb[:, 0, g, :], pT_sb[:, g % 2, 0:2, :].rearrange("p a k -> p (a k)"), start=True, stop=False)
                mm(ps[:, 7, P:TOK], v_sb[:, 1, g, :], pT_sb[:, g % 2, 2, :], start=False, stop=True).then_inc(ho_ps, 1)

            def head_out(g):
                pe.wait_ge(ho_ready, g + 1)
                pe.wait_ge(wout_lo_done, g + 1)
                for t in range(NT):
                    for part, wpart in ((0, 0), (1, 0), (0, 1)):
                        for a in range(2):
                            last = mm(ps[:, 2 * t + a, :], attn_s[part][:, g % 2, t * P:(t + 1) * P],
                                      wout_s[wpart][:, g % 2, a * HALF:(a + 1) * HALF],
                                      start=(g == 0 and part == 0 and wpart == 0), stop=(g == H - 1 and wpart == 1))
                last.then_inc(wout_used, 1)

            for s in range(H + 4):
                if s == 1:
                    turn_queries(1)
                    pe.wait_ge(kpeT_ready, 1)
                    pe.wait_ge(qpeT_ready, NT)
                for lag, stage in enumerate((head_project, head_scores, head_turn, head_values, head_out)):
                    if 0 <= s - lag < H:
                        stage(s - lag)

            pe.sem_inc(w_used, SPLIT)

            def gather(e):
                for c in range(NC):
                    for t in range(NT):
                        last = mm(ps[:, c // 4, (c % 4) * SLOTS:(c % 4 + 1) * SLOTS], fN[:, t, c * P:(c + 1) * P],
                                  sel[:, t, bass.ds(e * SLOTS, SLOTS)], start=(t == 0), stop=(t == NT - 1))
                last.then_inc(gather_ps, 1)

            def combine(e, rows, banks=(5, 6, 7, 5)):
                pe.wait_ge(y_ready, e + 1)
                pe.wait_ge(ct_ready, e + 1)
                for r in rows:
                    if banks[r] in banks[:r]:
                        pe.wait_ge(comb_added, 4 * e + 1)
                    for part in range(2):
                        last = mm(ps[:, banks[r], :], ct_e[:, (r // 2) * P:(r // 2 + 1) * P], y_s[part][:, r % 2, :],
                                  start=(part == 0), stop=(part == 1))
                    last.then_inc(comb_ps, 1)

            def adapter(e):
                pe.wait_ge(xs_ready, e + 1)
                pe.wait_ge(wd_in, 16 * e + 32)
                for c in range(NC):
                    last = mm(ps[0:AR, 7, 0:SLOTS], wd_sb[:, c, :], xs[:, c, :], start=(c == 0), stop=(c == NC - 1))
                last.then_inc(adapt_ps, 1)

            def half(e, n):
                (kind, k), x = ROUND[n // 2], n % 2
                hi, lo = (half_view(w[:, n % SPLIT, :], n) for w in w_s)
                if kind == "w2" and x == 0:
                    pe.wait_ge(hid_ready, STEPS * e + k + 1)
                if kind == "s2" and x == 0:
                    pe.wait_ge(shid_ready, 2 * e + 2)
                if kind == "w2" and k == 0 and x == 0:
                    pe.wait_ge(y_ready, e + 1)
                pe.wait_ge(w_lo_done, NHALF * e + n + 1)
                if kind == "w1":
                    to = ps[0:SLOTS, k % 2, :]
                    for c in range(4):
                        for part in range(2):
                            mm(to, xs_s[part][:, 4 * x + c, :], hi[:, c, :], start=(x == 0 and c == 0 and part == 0), stop=False)
                    for c in range(4):
                        last = mm(to, xs_s[0][:, 4 * x + c, :], lo[:, c, :], start=False, stop=(x == 1 and c == 3))
                elif kind == "w2":
                    for j in range(2):
                        for part in range(2):
                            for a in range(2):
                                mm(ps[0:SLOTS, 3 + a, :], hid_s[part][:, k % 2, 2 * x + j, :], hi[:, j, a * HALF:(a + 1) * HALF],
                                   start=(k == 0 and x == 0 and j == 0 and part == 0), stop=False)
                    for j in range(2):
                        for a in range(2):
                            last = mm(ps[0:SLOTS, 3 + a, :], hid_s[0][:, k % 2, 2 * x + j, :], lo[:, j, a * HALF:(a + 1) * HALF],
                                      start=False, stop=False)
                elif kind == "s1":
                    for j in range(2):
                        for c in range(NC):
                            for w, act_part in ((hi, 0), (hi, 1), (lo, 0)):
                                last = mm(ps[:, 5 + x, j * TOK:(j + 1) * TOK], w[:, c, j * P:(j + 1) * P],
                                          hT_s[act_part][:, c, :], start=(c == 0 and act_part == 0 and w is hi),
                                          stop=(c == NC - 1 and w is lo))
                else:
                    last_round = isinstance(e, int) and e == E - 1
                    if last_round and x == 0:
                        pe.wait_ge(swub_in, 32)
                        for r in range(2 * NT):
                            mm(ps[:, S_BANKS[r], :], gs[:, (r // 2) * P:(r // 2 + 1) * P], swub_sb[:, r % 2, :],
                               start=True, stop=False)
                    for w, parts in ((hi, (0, 1)), (lo, (0,))):
                        for j in range(2):
                            for part in parts:
                                for r in range(2 * NT):
                                    first = x == 0 and j == 0 and part == 0 and w is hi
                                    last = mm(ps[:, S_BANKS[r], :], shid_s[part][:, 2 * x + j, (r // 2) * P:(r // 2 + 1) * P],
                                              w[:, j, (r % 2) * HALF:(r % 2 + 1) * HALF],
                                              start=first and not last_round, stop=(x == 1 and j == 1 and w is lo))
                last.then_inc(w_used, 1)
                for q in range(STEPS):
                    if n == FIRST_HALF["w1", q] + 2:
                        pe.wait_ge(a_copied, STEPS * e + q + 1)
                        for j in range(4):
                            last = turn(ps[:, 2, j * SLOTS:(j + 1) * SLOTS], a_sb[:, j * P:(j + 1) * P], ident[0:SLOTS, 0:SLOTS])
                        last.then_inc(a_turned, 1)
                if n == COMBINE:
                    pe.wait_ge(ga_ready, e + 1)
                    pe.wait_ge(sgelu_done, e + 1)
                    combine(e, (0, 1, 2))
                if n == COMBINE + 3:
                    combine(e, (3,))
                if n == FIRST_HALF["s2", 0] - 1:
                    pe.wait_ge(comb_added, 4 * e + 4)
                if n == FIRST_HALF["w2", STEPS - 1] + 1:
                    pe.wait_ge(wub_in, 32 * e + 32)
                    for a in range(2):
                        last = mm(ps[0:SLOTS, 3 + a, :], ga, wub_sb[:, a, :], start=False, stop=True)
                    last.then_inc(y_ps, 1)

            layernorm_turn(2, fN)
            pe.wait_ge(gate_in, 16)
            for t in range(NT):
                for c in range(NC):
                    last = mm(ps[:, 4, t * E:(t + 1) * E], fT[:, c, t * P:(t + 1) * P], gate_sb[:, c, :],
                              start=(c == 0), stop=(c == NC - 1))
            last.then_inc(gate_ps, 1)
            pe.wait_ge(wd_in, 16)
            for c in range(NC):
                last = mm(ps[0:AR, 7, 0:TOK], wd_sb[:, c, :], fT[:, c, :], start=(c == 0), stop=(c == NC - 1))
            last.then_inc(adapt_ps, 1)
            pe.wait_ge(norm_lo, NT)
            half(0, 0)
            pe.wait_ge(onehot_ready, 1)
            n = E * TOPK
            mm(ps[:, 2, 0:n], upperb[:, :], onehotb[:, 0, :], start=True, stop=True)
            mm(ps[:, 2, n:2 * n], onesb[:, :], onehotb[:, 0, :], start=True, stop=False)
            mm(ps[:, 2, n:2 * n], upperb[:, :], onehotb[:, 1, :], start=False, stop=True).then_inc(pos_ps, 1)
            half(0, 1)
            pe.wait_ge(sel_ready, NT * TOPK)
            gather(0)
            pe.wait_ge(gs_ready, 1)
            for e in range(E):
                for t in range(NT):
                    at = (e % 2) * TOK + t * P
                    last = turn(ps[0:SLOTS, COMB_BANKS[e // 2], at:at + P],
                                sel[:, t, e * SLOTS:(e + 1) * SLOTS], ident)
                if e % 2:
                    last.then_inc(combT_ps, 1)
            pe.wait_ge(combT_ready, 1)
            for e in range(E):
                for t in range(NT):
                    last = mm(ps[0:SLOTS, 4, e:e + 1], selw[:, t, e * SLOTS:(e + 1) * SLOTS], onesf[:, 0:1],
                              start=(t == 0), stop=(t == NT - 1))
            last.then_inc(slot_w_ps, 1)
            pe.wait_ge(combT_ready, 4)
            adapter(0)

            with pe.Fori(0, E - 1) as e:
                for n in range(2, NHALF):
                    half(e, n)
                pe.wait_ge(sh_added, 4 * e + 5)
                gather(e + 1)
                for n in range(2):
                    half(e + 1, n)
                adapter(e + 1)
            for n in range(2, NHALF):
                half(E - 1, n)
            pe.wait_ge(sh_added, 4 * E + 1)
            combine(E, range(2 * NT), S_BANKS)


_INS = ['x', 'ctx_2048', 'mask', 'L0_attn_Wqa', 'L0_attn_Wqb', 'L0_attn_Wkva', 'L0_attn_Wkvb', 'L0_attn_Wout',
        'L0_ffn_gate_w', 'L0_ffn_w1', 'L0_ffn_b1', 'L0_ffn_w2', 'L0_ffn_b2', 'L0_ffn_wd', 'L0_ffn_wu', 'L0_ffn_sw1',
        'L0_ffn_sb1', 'L0_ffn_sw2', 'L0_ffn_sb2', 'L0_ffn_swd', 'L0_ffn_swu', 'consts']
_OUTS = [((1, TOK, D), 'float32')]


def constants(np):
    c = np.zeros((P, NCONST), np.float32)
    c[:, C_ID:C_ID + P] = np.eye(P)
    c[:, C_UP:C_UP + P] = np.triu(np.ones((P, P)), 1)
    c[:, C_CAUS:C_CAUS + P] = np.triu(np.full((P, P), NEG), 1)
    theta = np.float32(10000.0) ** (np.float32(-2.0) * np.arange(ROPE // 2, dtype=np.float32) / np.float32(ROPE))
    angle = (np.arange(TOK, dtype=np.float32)[:, None] * theta[None, :].astype(np.float32)).astype(np.float32)
    for t in range(NT):
        c[:, C_COS + 32 * t:C_COS + 32 * t + 32] = np.cos(angle[t * P:(t + 1) * P])
        c[:, C_SIN + 32 * t:C_SIN + 32 * t + 32] = np.sin(angle[t * P:(t + 1) * P])
    c[:, C_I8:C_I8 + E] = np.arange(E)
    c[:, C_I40:C_I40 + CAP] = np.arange(CAP)
    c[0:NBLK, C_BNO:C_BNO + NBLK] = np.diag(np.arange(1, NBLK + 1))
    return c


def kernel(**inputs):
    import numpy as _np
    import concourse.bacc as _bacc
    from concourse import mybir as _mybir
    from concourse.bass_utils import run_bass_kernel_spmd as _run

    given = dict(inputs)
    given['mask'] = _np.concatenate([_np.zeros(HALF, bool), _np.asarray(inputs['mask_BxS2_bk0']).reshape(-1)])
    given['ctx_2048'] = _np.asarray(inputs['ctx_2048']).reshape(KEYS, D)
    given['consts'] = constants(_np)
    nc = _bacc.Bacc("TRN2", target_bir_lowering=False, num_devices=1)
    arrays, args = {}, []
    for name in _INS:
        a = _np.ascontiguousarray(given[name])
        arrays[f"in_{name}_dram"] = a
        args.append(nc.dram_tensor(f"in_{name}_dram", a.shape, _mybir.dt.from_np(a.dtype), kind="ExternalInput").ap())
    for i, (shape, dtype) in enumerate(_OUTS):
        dt = _mybir.dt.from_np(_np.dtype(dtype))
        args.append(nc.dram_tensor(f"out_{i}_dram", shape, dt, kind="ExternalOutput").ap())
    build(nc, *args)
    r = _run(nc, [arrays], core_ids=[0])
    got = tuple(r.results[0][f"out_{i}_dram"] for i in range(len(_OUTS)))
    return got[0]
```
